# Optimizing a Trainium2 kernel written in Bass

```python
import numpy as np
import jax
import jax.numpy as jnp

def _softmax(x, axis=-1):
    return jax.nn.softmax(x, axis=axis)

def _gelu(x):
    return jax.nn.gelu(x, approximate=True)

def _silu(x):
    return jax.nn.silu(x)

def _sigmoid(x):
    return jax.nn.sigmoid(x)

def _layernorm(x, axis=-1, eps=1e-05):
    m = jnp.mean(x, axis=axis, keepdims=True)
    v = jnp.var(x, axis=axis, keepdims=True)
    return (x - m) / jnp.sqrt(v + eps)

def _scatter_add(tgt, idx, src, axis=0):
    return tgt.at[idx].add(src)

def _segment_sum(src, seg, n):
    return jax.ops.segment_sum(src, seg, n)
kernel_name = 'mk_recurrent_d2_jaxref_r4_ab9128'

def setup_inputs(seed: int=0):
    np.random.seed(seed)
    _w = jnp.asarray

    def _L0_attn_setup():
        import jax, jax.numpy as jnp
        import numpy as np
        import math
        B, N, D, H = (1, 1024, 256, 16)
        HS = D // H
        NEG_INF = -10000.0
        key = jax.random.key(seed)
        k1, k2, k3, k4, k5 = jax.random.split(key, 5)
        return {'encodings': jax.random.normal(k1, (B, N, D), dtype=jnp.float32), 'attn_W': jax.random.normal(k2, (D, 3 * D), dtype=jnp.float32) * 0.02, 'attn_b': jax.random.normal(k3, (3 * D,), dtype=jnp.float32) * 0.02, 'out_W': jax.random.normal(k4, (D, D), dtype=jnp.float32) * 0.02, 'out_b': jax.random.normal(k5, (D,), dtype=jnp.float32) * 0.02}
    _L0_attn_in = _L0_attn_setup()

    def _L0_ffn_setup():
        import jax, jax.numpy as jnp
        import numpy as np
        B, S, D = (4, 1024, 256)
        E, F_EXP = (16, 512)
        F_C = 2.0
        F_SH = 512
        key = jax.random.key(seed)
        ks = jax.random.split(key, 8)
        s = 0.02
        return {'hidden_states': jax.random.normal(ks[0], (B, S, D), jnp.float32), 'gate_w': jax.random.normal(ks[1], (E, D), jnp.float32) * s, 'Wg': jax.random.normal(ks[2], (E, F_EXP, D), jnp.float32) * s, 'Wu': jax.random.normal(ks[3], (E, F_EXP, D), jnp.float32) * s, 'Wd': jax.random.normal(ks[4], (E, D, F_EXP), jnp.float32) * s, 'Ws_g': jax.random.normal(ks[5], (F_SH, D), jnp.float32) * s, 'Ws_u': jax.random.normal(ks[6], (F_SH, D), jnp.float32) * s, 'Ws_d': jax.random.normal(ks[7], (D, F_SH), jnp.float32) * s}
    _L0_ffn_in = _L0_ffn_setup()

    def _L1_attn_setup():
        import jax, jax.numpy as jnp
        import numpy as np
        B, T, D = (2, 512, 256)
        H = 8
        KD = 128
        VD = 64
        KEY_DIM = H * KD
        VAL_DIM = H * VD
        KS = 4
        EPS_NORM = 1e-06
        EPS_RMS = 1e-05

        def _xavier(key, shape):
            fan_in, fan_out = (shape[0], shape[1])
            lim = np.sqrt(6.0 / (fan_in + fan_out))
            return jax.random.uniform(key, shape, jnp.float32, -lim, lim)

        def _causal_dw_conv_silu(x, w):
            C = x.shape[-1]
            y = jax.lax.conv_general_dilated(jnp.swapaxes(x, 1, 2), w[:, None, :], window_strides=(1,), padding=[(KS - 1, 0)], feature_group_count=C)
            return jax.nn.silu(jnp.swapaxes(y, 1, 2))

        def _l2norm(x):
            n = jnp.sqrt(jnp.sum(x * x, axis=-1, keepdims=True))
            return x / jnp.maximum(n, EPS_NORM)

        def _gdn_forward(x, Wq, Wk, Wv, Wa, Wb, Wg, Wo, A_log, dt_bias, conv_q, conv_k, conv_v, o_norm_w):
            bsz, seq_len, _ = x.shape
            beta = jax.nn.sigmoid(x @ Wb) * 2.0
            g = -jnp.exp(A_log)[None, None, :] * jax.nn.softplus(x @ Wa + dt_bias[None, None, :])
            alpha = jnp.exp(g)
            q = _causal_dw_conv_silu(x @ Wq, conv_q).reshape(bsz, seq_len, H, KD)
            k = _causal_dw_conv_silu(x @ Wk, conv_k).reshape(bsz, seq_len, H, KD)
            v = _causal_dw_conv_silu(x @ Wv, conv_v).reshape(bsz, seq_len, H, VD)
            q = _l2norm(q)
            k = _l2norm(k)
            qT = jnp.swapaxes(q, 0, 1)
            kT = jnp.swapaxes(k, 0, 1)
            vT = jnp.swapaxes(v, 0, 1)
            aT = jnp.swapaxes(alpha, 0, 1)
            bT = jnp.swapaxes(beta, 0, 1)

            def step(state, inp):
                q_t, k_t, v_t, a_t, b_t = inp
                retained = jnp.einsum('bhvk,bhk->bhv', state, k_t)
                a4 = a_t[..., None, None]
                b4 = b_t[..., None, None]
                rk = retained[..., None] * k_t[:, :, None, :]
                vk = v_t[..., None] * k_t[:, :, None, :]
                state = a4 * (state - b4 * rk) + b4 * vk
                o_t = jnp.einsum('bhvk,bhk->bhv', state, q_t)
                return (state, o_t)
            state0 = jnp.zeros((bsz, H, VD, KD), jnp.float32)
            _, outT = jax.lax.scan(step, state0, (qT, kT, vT, aT, bT))
            out = jnp.swapaxes(outT, 0, 1)
            gate = (x @ Wg).reshape(bsz, seq_len, H, VD)
            rms = jax.lax.rsqrt(jnp.mean(out * out, axis=-1, keepdims=True) + EPS_RMS)
            out = out * rms * o_norm_w * jax.nn.silu(gate)
            out = out.reshape(bsz, seq_len, VAL_DIM)
            return out @ Wo
        key = jax.random.key(seed)
        ks = jax.random.split(key, 16)
        x = jax.random.normal(ks[0], (B, T, D), jnp.float32)
        Wq = _xavier(ks[1], (D, KEY_DIM))
        Wk = _xavier(ks[2], (D, KEY_DIM))
        Wv = _xavier(ks[3], (D, VAL_DIM))
        Wa = _xavier(ks[4], (D, H))
        Wb = _xavier(ks[5], (D, H))
        Wg = _xavier(ks[6], (D, VAL_DIM))
        Wo = _xavier(ks[7], (VAL_DIM, D))
        A_log = jnp.log(jax.random.uniform(ks[8], (H,), jnp.float32, 0.5, 16.0))
        dt = jnp.exp(jax.random.uniform(ks[9], (H,), jnp.float32, np.log(0.001), np.log(0.1)))
        dt = jnp.clip(dt, 0.0001, None)
        dt_bias = dt + jnp.log(-jnp.expm1(-dt))

        def conv_w(k, c):
            lim = np.sqrt(6.0 / (1 + KS))
            return jax.random.uniform(k, (c, KS), jnp.float32, -lim, lim)
        conv_q = conv_w(ks[10], KEY_DIM)
        conv_k = conv_w(ks[11], KEY_DIM)
        conv_v = conv_w(ks[12], VAL_DIM)
        o_norm_w = jnp.ones((VD,), jnp.float32)
        return dict(x=x, Wq=Wq, Wk=Wk, Wv=Wv, Wa=Wa, Wb=Wb, Wg=Wg, Wo=Wo, A_log=A_log, dt_bias=dt_bias, conv_q=conv_q, conv_k=conv_k, conv_v=conv_v, o_norm_w=o_norm_w)
    _L1_attn_in = _L1_attn_setup()

    def _L1_ffn_setup():
        import jax, jax.numpy as jnp
        import numpy as np
        HIDDEN = 256
        N_ROUTED = 16
        N_SHARED = 2
        TOP_K = 2
        MID_R = HIDDEN // 4
        MID_S = HIDDEN // 2
        key = jax.random.key(seed)
        ks = jax.random.split(key, 8)
        s = 0.02
        return {'x': jax.random.normal(ks[0], (2, 256, HIDDEN), dtype=jnp.float32), 'router_w': jax.random.normal(ks[1], (HIDDEN, N_ROUTED), dtype=jnp.float32) * s, 'wg_r': jax.random.normal(ks[2], (N_ROUTED, HIDDEN, MID_R), dtype=jnp.float32) * s, 'wu_r': jax.random.normal(ks[3], (N_ROUTED, HIDDEN, MID_R), dtype=jnp.float32) * s, 'wd_r': jax.random.normal(ks[4], (N_ROUTED, MID_R, HIDDEN), dtype=jnp.float32) * s, 'wg_s': jax.random.normal(ks[5], (N_SHARED, HIDDEN, MID_S), dtype=jnp.float32) * s, 'wu_s': jax.random.normal(ks[6], (N_SHARED, HIDDEN, MID_S), dtype=jnp.float32) * s, 'wd_s': jax.random.normal(ks[7], (N_SHARED, MID_S, HIDDEN), dtype=jnp.float32) * s}
    _L1_ffn_in = _L1_ffn_setup()
    _d = {'L0_attn_encodings': _L0_attn_in['encodings'], 'L0_attn_attn_W': _L0_attn_in['attn_W'], 'L0_attn_attn_b': _L0_attn_in['attn_b'], 'L0_attn_out_W': _L0_attn_in['out_W'], 'L0_attn_out_b': _L0_attn_in['out_b'], 'L0_ffn_gate_w': _L0_ffn_in['gate_w'], 'L0_ffn_Wg': _L0_ffn_in['Wg'], 'L0_ffn_Wu': _L0_ffn_in['Wu'], 'L0_ffn_Wd': _L0_ffn_in['Wd'], 'L0_ffn_Ws_g': _L0_ffn_in['Ws_g'], 'L0_ffn_Ws_u': _L0_ffn_in['Ws_u'], 'L0_ffn_Ws_d': _L0_ffn_in['Ws_d'], 'L1_attn_Wq': _L1_attn_in['Wq'], 'L1_attn_Wk': _L1_attn_in['Wk'], 'L1_attn_Wv': _L1_attn_in['Wv'], 'L1_attn_Wa': _L1_attn_in['Wa'], 'L1_attn_Wb': _L1_attn_in['Wb'], 'L1_attn_Wg': _L1_attn_in['Wg'], 'L1_attn_Wo': _L1_attn_in['Wo'], 'L1_attn_A_log': _L1_attn_in['A_log'], 'L1_attn_dt_bias': _L1_attn_in['dt_bias'], 'L1_attn_conv_q': _L1_attn_in['conv_q'], 'L1_attn_conv_k': _L1_attn_in['conv_k'], 'L1_attn_conv_v': _L1_attn_in['conv_v'], 'L1_attn_o_norm_w': _L1_attn_in['o_norm_w'], 'L1_ffn_router_w': _L1_ffn_in['router_w'], 'L1_ffn_wg_r': _L1_ffn_in['wg_r'], 'L1_ffn_wu_r': _L1_ffn_in['wu_r'], 'L1_ffn_wd_r': _L1_ffn_in['wd_r'], 'L1_ffn_wg_s': _L1_ffn_in['wg_s'], 'L1_ffn_wu_s': _L1_ffn_in['wu_s'], 'L1_ffn_wd_s': _L1_ffn_in['wd_s']}
    _x0 = _d['L0_attn_encodings']
    _d['L0_attn_encodings'] = jax.random.normal(jax.random.fold_in(jax.random.key(seed), 1), (8, 1024, 256), dtype=_x0.dtype)
    del _x0
    return _d

def reference(L0_attn_encodings, L0_attn_attn_W, L0_attn_attn_b, L0_attn_out_W, L0_attn_out_b, L0_ffn_gate_w, L0_ffn_Wg, L0_ffn_Wu, L0_ffn_Wd, L0_ffn_Ws_g, L0_ffn_Ws_u, L0_ffn_Ws_d, L1_attn_Wq, L1_attn_Wk, L1_attn_Wv, L1_attn_Wa, L1_attn_Wb, L1_attn_Wg, L1_attn_Wo, L1_attn_A_log, L1_attn_dt_bias, L1_attn_conv_q, L1_attn_conv_k, L1_attn_conv_v, L1_attn_o_norm_w, L1_ffn_router_w, L1_ffn_wg_r, L1_ffn_wu_r, L1_ffn_wd_r, L1_ffn_wg_s, L1_ffn_wu_s, L1_ffn_wd_s):

    def _L0_attn_ref(encodings, attn_W, attn_b, out_W, out_b):
        import jax, jax.numpy as jnp
        import numpy as np
        import math
        B, N, D, H = (1, 1024, 256, 16)
        HS = D // H
        NEG_INF = -10000.0
        b, n, d = encodings.shape
        qkv = encodings @ attn_W + attn_b
        qkv = qkv.reshape(b, n, H, 3 * HS).transpose(0, 2, 1, 3)
        q, k, v = jnp.split(qkv, 3, axis=-1)
        scores = jnp.einsum('bhki,bhqi->bhkq', k, q) / math.sqrt(HS)
        mask = jnp.arange(n)[:, None] <= jnp.arange(n)[None, :]
        scores = jnp.where(mask, scores, jnp.float32(NEG_INF))
        prob = jax.nn.softmax(scores, axis=2)
        combined = jnp.einsum('bhkq,bhkl->bhql', prob, v)
        out = combined.transpose(0, 2, 1, 3).reshape(b, n, d)
        return out @ out_W + out_b

    def _L0_ffn_ref(hidden_states, gate_w, Wg, Wu, Wd, Ws_g, Ws_u, Ws_d):
        import jax, jax.numpy as jnp
        import numpy as np
        B, S, D = (4, 1024, 256)
        E, F_EXP = (16, 512)
        F_C = 2.0
        F_SH = 512
        b, s, d = hidden_states.shape
        e = gate_w.shape[0]
        cap = int(s * F_C / e)
        logits = jnp.einsum('bsd,ed->bse', hidden_states, gate_w)
        scores = jax.nn.softmax(logits, axis=-1).transpose(0, 2, 1)
        topk_w, topk_idx = jax.lax.top_k(scores, cap)
        x_tok = jnp.take_along_axis(hidden_states[:, None, :, :], topk_idx[..., None], axis=2)
        g = jnp.einsum('becd,efd->becf', x_tok, Wg)
        u = jnp.einsum('becd,efd->becf', x_tok, Wu)
        h = jax.nn.gelu(g, approximate=False) * u
        eo = jnp.einsum('becf,edf->becd', h, Wd) * topk_w[..., None]
        offs = (jnp.arange(b) * s)[:, None, None]
        flat_idx = (topk_idx + offs).reshape(-1)
        flat = jnp.zeros((b * s, d), hidden_states.dtype)
        flat = flat.at[flat_idx].add(eo.reshape(-1, d))
        out = flat.reshape(b, s, d)
        gs = jnp.einsum('bsd,fd->bsf', hidden_states, Ws_g)
        us = jnp.einsum('bsd,fd->bsf', hidden_states, Ws_u)
        shared = jnp.einsum('bsf,df->bsd', jax.nn.gelu(gs, approximate=False) * us, Ws_d)
        return out + shared

    def _L1_attn_ref(x, Wq, Wk, Wv, Wa, Wb, Wg, Wo, A_log, dt_bias, conv_q, conv_k, conv_v, o_norm_w):
        import jax, jax.numpy as jnp
        import numpy as np
        B, T, D = (2, 512, 256)
        H = 8
        KD = 128
        VD = 64
        KEY_DIM = H * KD
        VAL_DIM = H * VD
        KS = 4
        EPS_NORM = 1e-06
        EPS_RMS = 1e-05

        def _xavier(key, shape):
            fan_in, fan_out = (shape[0], shape[1])
            lim = np.sqrt(6.0 / (fan_in + fan_out))
            return jax.random.uniform(key, shape, jnp.float32, -lim, lim)

        def _causal_dw_conv_silu(x, w):
            C = x.shape[-1]
            y = jax.lax.conv_general_dilated(jnp.swapaxes(x, 1, 2), w[:, None, :], window_strides=(1,), padding=[(KS - 1, 0)], feature_group_count=C)
            return jax.nn.silu(jnp.swapaxes(y, 1, 2))

        def _l2norm(x):
            n = jnp.sqrt(jnp.sum(x * x, axis=-1, keepdims=True))
            return x / jnp.maximum(n, EPS_NORM)

        def _gdn_forward(x, Wq, Wk, Wv, Wa, Wb, Wg, Wo, A_log, dt_bias, conv_q, conv_k, conv_v, o_norm_w):
            bsz, seq_len, _ = x.shape
            beta = jax.nn.sigmoid(x @ Wb) * 2.0
            g = -jnp.exp(A_log)[None, None, :] * jax.nn.softplus(x @ Wa + dt_bias[None, None, :])
            alpha = jnp.exp(g)
            q = _causal_dw_conv_silu(x @ Wq, conv_q).reshape(bsz, seq_len, H, KD)
            k = _causal_dw_conv_silu(x @ Wk, conv_k).reshape(bsz, seq_len, H, KD)
            v = _causal_dw_conv_silu(x @ Wv, conv_v).reshape(bsz, seq_len, H, VD)
            q = _l2norm(q)
            k = _l2norm(k)
            qT = jnp.swapaxes(q, 0, 1)
            kT = jnp.swapaxes(k, 0, 1)
            vT = jnp.swapaxes(v, 0, 1)
            aT = jnp.swapaxes(alpha, 0, 1)
            bT = jnp.swapaxes(beta, 0, 1)

            def step(state, inp):
                q_t, k_t, v_t, a_t, b_t = inp
                retained = jnp.einsum('bhvk,bhk->bhv', state, k_t)
                a4 = a_t[..., None, None]
                b4 = b_t[..., None, None]
                rk = retained[..., None] * k_t[:, :, None, :]
                vk = v_t[..., None] * k_t[:, :, None, :]
                state = a4 * (state - b4 * rk) + b4 * vk
                o_t = jnp.einsum('bhvk,bhk->bhv', state, q_t)
                return (state, o_t)
            state0 = jnp.zeros((bsz, H, VD, KD), jnp.float32)
            _, outT = jax.lax.scan(step, state0, (qT, kT, vT, aT, bT))
            out = jnp.swapaxes(outT, 0, 1)
            gate = (x @ Wg).reshape(bsz, seq_len, H, VD)
            rms = jax.lax.rsqrt(jnp.mean(out * out, axis=-1, keepdims=True) + EPS_RMS)
            out = out * rms * o_norm_w * jax.nn.silu(gate)
            out = out.reshape(bsz, seq_len, VAL_DIM)
            return out @ Wo
        return _gdn_forward(x, Wq, Wk, Wv, Wa, Wb, Wg, Wo, A_log, dt_bias, conv_q, conv_k, conv_v, o_norm_w)

    def _L1_ffn_ref(x, router_w, wg_r, wu_r, wd_r, wg_s, wu_s, wd_s):
        import jax, jax.numpy as jnp
        import numpy as np
        HIDDEN = 256
        N_ROUTED = 16
        N_SHARED = 2
        TOP_K = 2
        MID_R = HIDDEN // 4
        MID_S = HIDDEN // 2
        orig_shape = x.shape
        flat = x.reshape(-1, orig_shape[-1])
        gs = jnp.einsum('td,ndm->tnm', flat, wg_s)
        us = jnp.einsum('td,ndm->tnm', flat, wu_s)
        out = jnp.einsum('tnm,nmd->td', jax.nn.silu(gs) * us, wd_s)
        logits = (flat @ router_w).astype(jnp.float32)
        probs = jax.nn.softmax(logits, axis=-1)
        weights, indices = jax.lax.top_k(probs, TOP_K)
        weights = weights / (weights.sum(axis=-1, keepdims=True) + 1e-09)
        weights = weights.astype(x.dtype)
        comb = jnp.sum(jax.nn.one_hot(indices, N_ROUTED, dtype=x.dtype) * weights[..., None], axis=1)
        g = jnp.einsum('td,edm->tem', flat, wg_r)
        u = jnp.einsum('td,edm->tem', flat, wu_r)
        h = jax.nn.silu(g) * u
        h = h * comb[:, :, None]
        out = out + jnp.einsum('tem,emd->td', h, wd_r)
        return out.reshape(orig_shape)
    x = L0_attn_encodings
    xn = _layernorm(x, axis=-1)
    s = _L0_attn_ref(xn, L0_attn_attn_W, L0_attn_attn_b, L0_attn_out_W, L0_attn_out_b)
    g = _silu(_L0_ffn_ref(xn, L0_ffn_gate_w, L0_ffn_Wg, L0_ffn_Wu, L0_ffn_Wd, L0_ffn_Ws_g, L0_ffn_Ws_u, L0_ffn_Ws_d))
    x = x + s * g
    xn = _layernorm(x, axis=-1)
    s = _L1_attn_ref(xn, L1_attn_Wq, L1_attn_Wk, L1_attn_Wv, L1_attn_Wa, L1_attn_Wb, L1_attn_Wg, L1_attn_Wo, L1_attn_A_log, L1_attn_dt_bias, L1_attn_conv_q, L1_attn_conv_k, L1_attn_conv_v, L1_attn_o_norm_w)
    g = _silu(_L1_ffn_ref(xn, L1_ffn_router_w, L1_ffn_wg_r, L1_ffn_wu_r, L1_ffn_wd_r, L1_ffn_wg_s, L1_ffn_wu_s, L1_ffn_wd_s))
    x = x + s * g
    return x

_drawn_inputs = setup_inputs


def setup_inputs(seed=0):
    import zlib

    import numpy as np

    out = dict(_drawn_inputs(seed))
    spreads = {'L1_attn_o_norm_w': (1.0, 0.6)}
    factors = {'L0_attn_attn_W': 8.0,
     'L0_attn_attn_b': 8.0,
     'L0_attn_out_W': 8.0,
     'L0_attn_out_b': 8.0,
     'L0_ffn_gate_w': 8.0,
     'L0_ffn_Wg': 8.0,
     'L0_ffn_Wu': 8.0,
     'L0_ffn_Wd': 8.0,
     'L0_ffn_Ws_g': 8.0,
     'L0_ffn_Ws_u': 8.0,
     'L0_ffn_Ws_d': 8.0,
     'L1_attn_Wq': 8.0,
     'L1_attn_Wk': 8.0,
     'L1_attn_Wv': 8.0,
     'L1_attn_Wa': 8.0,
     'L1_attn_Wb': 8.0,
     'L1_attn_Wg': 8.0,
     'L1_attn_Wo': 8.0,
     'L1_attn_A_log': 8.0,
     'L1_attn_dt_bias': 8.0,
     'L1_attn_conv_q': 8.0,
     'L1_attn_conv_k': 8.0,
     'L1_attn_conv_v': 8.0,
     'L1_ffn_router_w': 8.0,
     'L1_ffn_wg_r': 8.0,
     'L1_ffn_wu_r': 8.0,
     'L1_ffn_wd_r': 8.0,
     'L1_ffn_wg_s': 8.0,
     'L1_ffn_wu_s': 8.0,
     'L1_ffn_wd_s': 8.0}
    for name, (base, spread) in spreads.items():
        noise = np.random.default_rng([zlib.crc32(name.encode()), seed]).standard_normal(out[name].shape)
        drawn = base * np.exp(spread * noise) if base else spread * noise
        out[name] = jnp.asarray(drawn.astype(out[name].dtype))
    for name, factor in factors.items():
        out[name] = (out[name] * factor).astype(out[name].dtype)
    return out
```

```python
from contextlib import ExitStack

import numpy as np

import concourse.bass as bass
from concourse import mybir

P = 128
ALU = mybir.AluOpType
AF = mybir.ActivationFunctionType
F32 = mybir.dt.float32
BF16 = mybir.dt.bfloat16
U32 = mybir.dt.uint32
I32 = mybir.dt.int32
AX = mybir.AxisListType
LEAST_LOGIT = -46.0

def this(turn, per, k=None):
    return turn * per + (per + (per if k is None else k))


def last(turn, per, k=None):
    return turn * per + (per if k is None else k)


def after(eng, step, instruction):
    instruction.then_inc(step, 1)
    eng.wait_ge(step, 1)
    eng.sem_inc(step, -1)


def _memory(nc, ctx, prefix):
    sems = []

    def clear():
        nc.clear_and_free_semaphores(sems)
        nc.all_engine_barrier()

    ctx.callback(clear)

    def sb(name, shape, dt=F32):
        return ctx.enter_context(nc.sbuf_tensor(prefix + name, shape, dt))

    def ps(name, shape, dt=F32):
        return ctx.enter_context(nc.psum_tensor(prefix + name, shape, dt))

    def sem(name):
        sems.append(nc.alloc_semaphore(prefix + name))
        return sems[-1]

    return sb, ps, sem


def project_l0(nc, x, w, xn_d, qk_d, v_d, score_d, ffn_d):
    B, N, D = x.shape
    C = 512
    T = C // P
    K2 = D // P
    NH, HS, NE, NF = 16, D // 16, 16, 4
    with ExitStack() as ctx:
        sb, ps, sem = _memory(nc, ctx, "a_")
        ident = sb("ident", [P, P])
        wqk = sb("wqk", [P, K2, 4, P])
        bqk = sb("bqk", [P, 4])
        wv = sb("wv", [P, K2, D])
        bv = sb("bv", [P, D])
        wr = sb("wr", [P, K2, NE])
        wg = sb("wg", [P, K2, NF, P])
        wu = sb("wu", [P, K2, NF, P])
        wd = sb("wd", [P, NF, D])
        minus_half = sb("minus_half", [P, T])
        xin = sb("xin", [P, 2, T, D])
        stats = sb("stats", [P, T, 6])
        mv = sb("mv", [P, T, 2])
        veps = sb("veps", [P, T])
        rstd = sb("rstd", [P, T])
        xn = sb("xn", [P, T, D])
        xnT = sb("xnT", [P, K2, C])
        qf = sb("qf", [P, 2, C])
        qr = sb("qr", [P, C])
        parts = sb("parts", [P, 4, 3, C], BF16)
        vo = sb("vo", [P, T, NH, HS + 1])
        lg = sb("lg", [P, T, NE])
        le = sb("le", [P, T, NE])
        pr = sb("pr", [P, T, NE])
        lm = sb("lm", [P, T])
        scT = sb("scT", [NE, C])
        gel = sb("gel", [P, 2, C])
        hid = sb("hid", [P, NF, C])
        fo = sb("fo", [P, T, D])
        pT = ps("pT", [P, K2, C])
        pQ = ps("pQ", [P, 2, C])
        pG = ps("pG", [P, C])
        pU = ps("pU", [P, C])
        pL = ps("pL", [P, C])
        pS = ps("pS", [NE, C])

        weights_in, x_in = sem("weights_in"), [sem("x_in0"), sem("x_in1")]
        dve_step, act_step, pool_step = sem("dve_step"), sem("act_step"), sem("pool_step")
        var_ready, rstd_ready, xn_ready, xn_stored = sem("var_ready"), sem("rstd_ready"), sem("xn_ready"), sem("xn_stored")
        turned, xnT_ready = sem("turned"), sem("xnT_ready")
        qk_made, qk_copied, qk_split, qk_stored = sem("qk_made"), sem("qk_copied"), sem("qk_split"), sem("qk_stored")
        v_made, v_ready, v_stored = sem("v_made"), sem("v_ready"), sem("v_stored")
        l_made, l_shifted, l_exp, pr_ready = sem("l_made"), sem("l_shifted"), sem("l_exp"), sem("pr_ready")
        pr_turned, sc_ready, sc_stored = sem("pr_turned"), sem("sc_ready"), sem("sc_stored")
        g_made, gelu_done, u_made, hid_ready = sem("g_made"), sem("gelu_done"), sem("u_made"), sem("hid_ready")
        d_made, fo_ready, fo_stored = sem("d_made"), sem("fo_ready"), sem("fo_stored")
        block = ctx.enter_context(nc.Block())

        xt = x.rearrange("b (c t p) d -> b c p t d", c=2, p=P)
        xnt = xn_d.rearrange("(b c t p) d -> b c p t d", b=B, c=2, p=P)
        ft = ffn_d.rearrange("(b c t p) d -> b c p t d", b=B, c=2, p=P)
        vt = v_d.rearrange("b (c t p) e -> b c p t e", c=2, p=P)
        qkt = qk_d.rearrange("b s r (j p) n -> b s j p r n", p=P)
        consts = ((ident, "ident"), (wqk, "wqk"), (bqk, "bqk"), (wv, "wv"), (bv, "bv"),
                  (wr, "wr"), (wg, "wg"), (wu, "wu"), (wd, "wd"))

        @block.sync
        def _(sp):
            for q, per in ((xn_stored, 16), (qk_stored, 64), (v_stored, 16), (fo_stored, 16)):
                sp.sem_inc(q, per)
            for dst, name in consts:
                sp.dma_start(dst[:], w[name]).then_inc(weights_in, 16)
            with sp.Fori(0, B) as b:
                for s in range(2):
                    n = b * 2 + s
                    sp.wait_ge(xn_ready, this(n, 1))
                    sp.dma_start(xnt[b, s], xn[:]).then_inc(xn_stored, 16)
                    for j in range(4):
                        sp.wait_ge(qk_split, this(n, 4, j + 1))
                        sp.dma_start(qkt[b, j // 2, j % 2, :, :, s * C:(s + 1) * C], parts[:, j]).then_inc(qk_stored, 16)
                    sp.wait_ge(v_ready, this(n, T))
                    sp.dma_start(vt[b, s], vo[:].rearrange("p t h e -> p t (h e)")).then_inc(v_stored, 16)
                    sp.wait_ge(fo_ready, this(n, T))
                    sp.dma_start(ft[b, s], fo[:]).then_inc(fo_stored, 16)
            sp.wait_ge(xn_stored, this(2 * B - 1, 16))
            sp.wait_ge(qk_stored, this(2 * B - 1, 64))
            sp.wait_ge(v_stored, this(2 * B - 1, 16))
            sp.wait_ge(fo_stored, this(2 * B - 1, 16))

        @block.gpsimd
        def _(pool):
            pool.sem_inc(rstd_ready, 1)
            after(pool, pool_step, pool.memset(minus_half[:], -0.5))
            with pool.Fori(0, B) as b:
                for s in range(2):
                    n = b * 2 + s
                    pool.wait_ge(xn_ready, last(n, 1))
                    pool.dma_start(xin[:, s], xt[b, s]).then_inc(x_in[s], 16)
                    pool.wait_ge(var_ready, this(n, 1))
                    pool.tensor_tensor(rstd[:], veps[:], minus_half[:], ALU.pow).then_inc(rstd_ready, 1)

        @block.tensor
        def _(pe):
            for q, per in ((turned, 1), (qk_made, 4), (v_made, T), (l_made, 1), (pr_turned, 1), (g_made, NF), (u_made, NF), (d_made, T)):
                pe.sem_inc(q, per)
            pe.wait_ge(weights_in, 16 * len(consts))
            with pe.Fori(0, B) as b:
                for s in range(2):
                    n = b * 2 + s
                    pe.wait_ge(xn_ready, this(n, 1))
                    for k in range(K2):
                        for t in range(T):
                            mm = pe.transpose(pT[:, k, t * P:(t + 1) * P], xn[:, t, k * P:(k + 1) * P], ident[:])
                    mm.then_inc(turned, 1)
                    pe.wait_ge(xnT_ready, this(n, 1))
                    pe.wait_ge(l_shifted, last(n, 1))
                    for t in range(T):
                        for k in range(K2):
                            mm = pe.matmul(pL[:, t * NE:(t + 1) * NE], xnT[:, k, t * P:(t + 1) * P], wr[:, k, :],
                                           start=k == 0, stop=k == K2 - 1)
                    mm.then_inc(l_made, 1)
                    for j in range(4):
                        if j < 2:
                            pe.wait_ge(fo_ready, last(n, T, T - 1 + j))
                        else:
                            pe.wait_ge(qk_copied, this(n, 4, j - 1))
                        for k in range(K2):
                            mm = pe.matmul(pQ[:, j % 2], wqk[:, k, j, :], xnT[:, k, :], start=k == 0, stop=k == K2 - 1)
                        mm.then_inc(qk_made, 1)
                    for t in range(T):
                        if t < 2:
                            pe.wait_ge(qk_copied, this(n, 4, 3 + t))
                        else:
                            pe.wait_ge(v_ready, this(n, T, t - 1))
                        for k in range(K2):
                            mm = pe.matmul(pQ[:, t % 2, 0:D], xnT[:, k, t * P:(t + 1) * P], wv[:, k, :], start=k == 0, stop=k == K2 - 1)
                        mm.then_inc(v_made, 1)
                    pe.wait_ge(pr_ready, this(n, 1))
                    pe.wait_ge(sc_ready, last(n, 1))
                    for t in range(T):
                        mm = pe.transpose(pS[:, t * P:(t + 1) * P], pr[:, t, :], ident[:])
                    mm.then_inc(pr_turned, 1)
                    for f in range(NF):
                        pe.wait_ge(gelu_done, this(n, NF, f))
                        for k in range(K2):
                            mm = pe.matmul(pG[:], wg[:, k, f, :], xnT[:, k, :], start=k == 0, stop=k == K2 - 1)
                        mm.then_inc(g_made, 1)
                        pe.wait_ge(hid_ready, this(n, NF, f))
                        for k in range(K2):
                            mm = pe.matmul(pU[:], wu[:, k, f, :], xnT[:, k, :], start=k == 0, stop=k == K2 - 1)
                        mm.then_inc(u_made, 1)
                    pe.wait_ge(hid_ready, this(n, NF))
                    for t in range(T):
                        pe.wait_ge(*((v_ready, this(n, T, T - 1 + t)) if t < 2 else (fo_ready, this(n, T, t - 1))))
                        for f in range(NF):
                            mm = pe.matmul(pQ[:, t % 2, 0:D], hid[:, f, t * P:(t + 1) * P], wd[:, f, :], start=f == 0, stop=f == NF - 1)
                        mm.then_inc(d_made, 1)

        @block.scalar
        def _(act):
            for q, per in ((xnT_ready, 1), (qk_copied, 4), (l_exp, 1), (sc_ready, 1), (sc_stored, 16), (gelu_done, NF)):
                act.sem_inc(q, per)
            act.wait_ge(weights_in, 16 * len(consts))
            after(act, act_step, act.mul(bqk[:, 0:2], bqk[:, 0:2], HS ** -0.5))
            with act.Fori(0, B) as b:
                for s in range(2):
                    n = b * 2 + s
                    act.wait_ge(turned, this(n, 1))
                    act.wait_ge(u_made, last(n, NF))
                    for k in range(K2):
                        cp = act.copy(xnT[:, k], pT[:, k])
                    cp.then_inc(xnT_ready, 1)
                    act.wait_ge(l_shifted, this(n, 1))
                    act.wait_ge(pr_ready, last(n, 1))
                    act.activation(le[:], lg[:], AF.Exp).then_inc(l_exp, 1)
                    for j in range(4):
                        act.wait_ge(qk_made, this(n, 4, j + 1))
                        act.wait_ge(qk_split, this(n, 4, j - 1))
                        scale = HS ** -0.5 if j < 2 else 1.0
                        act.activation(qf[:, j % 2], pQ[:, j % 2], AF.Identity, bias=bqk[:, j:j + 1], scale=scale)
                        if j == 0:
                            act.wait_ge(qk_stored, last(n, 64))
                        act.activation(parts[:, j, 0], pQ[:, j % 2], AF.Identity, bias=bqk[:, j:j + 1],
                                       scale=scale).then_inc(qk_copied, 1)
                    act.wait_ge(pr_turned, this(n, 1))
                    act.wait_ge(sc_stored, last(n, 16))
                    act.copy(scT[:], pS[:]).then_inc(sc_ready, 1)
                    act.wait_ge(sc_ready, this(n, 1))
                    act.dma_start(score_d[b, :, s * C:(s + 1) * C], scT[:]).then_inc(sc_stored, 16)
                    for f in range(NF):
                        act.wait_ge(g_made, this(n, NF, f + 1))
                        act.wait_ge(hid_ready, this(n, NF, f - 1))
                        act.activation(gel[:, f % 2], pG[:], AF.Gelu).then_inc(gelu_done, 1)
            act.wait_ge(sc_stored, this(2 * B - 1, 16))

        @block.vector
        def _(dve):
            for q, per in ((var_ready, 1), (xn_ready, 1), (qk_split, 4), (v_ready, T), (l_shifted, 1), (pr_ready, 1),
                           (hid_ready, NF), (fo_ready, T)):
                dve.sem_inc(q, per)
            dve.memset(vo[:], 1.0)
            dve.wait_ge(weights_in, 16 * len(consts))
            with dve.Fori(0, B) as b:
                for s in range(2):
                    n = b * 2 + s
                    dve.wait_ge(x_in[s], b * 16 + 16)
                    for t in range(T):
                        st = dve.bn_stats(stats[:, t], xin[:, s, t])
                    after(dve, dve_step, st)
                    for t in range(T):
                        st = dve.bn_aggr(mv[:, t], stats[:, t])
                    after(dve, dve_step, st)
                    dve.tensor_scalar_add(veps[:], mv[:, :, 1], 1e-5).then_inc(var_ready, 1)
                    dve.wait_ge(turned, last(n, 1))
                    dve.wait_ge(xn_stored, last(n, 16))
                    dve.wait_ge(rstd_ready, this(n, 1))
                    for t in range(T):
                        st = dve.tensor_scalar(xn[:, t], xin[:, s, t], mv[:, t, 0:1], rstd[:, t:t + 1], ALU.subtract, ALU.mult)
                    st.then_inc(xn_ready, 1)
                    dve.wait_ge(l_made, this(n, 1))
                    pl = pL[:, 0:T * NE].rearrange("p (t e) -> p t e", t=T)
                    after(dve, dve_step, dve.tensor_reduce(lm[:], pl, AX.X, ALU.max))
                    dve.tensor_tensor(lg[:], pl, lm[:].unsqueeze(2).to_broadcast([P, T, NE]), ALU.subtract).then_inc(l_shifted, 1)
                    for j in range(4):
                        dve.wait_ge(qk_copied, this(n, 4, j + 1))
                        dve.wait_ge(qk_split, this(n, 4, j))
                        after(dve, dve_step, dve.tensor_tensor(qr[:], qf[:, j % 2], parts[:, j, 0], ALU.subtract))
                        after(dve, dve_step, dve.tensor_copy(parts[:, j, 1], qr[:]))
                        dve.tensor_tensor(parts[:, j, 2], qr[:], parts[:, j, 1], ALU.subtract).then_inc(qk_split, 1)
                        if j == 0:
                            dve.wait_ge(l_exp, this(n, 1))
                            after(dve, dve_step, dve.tensor_reduce(lm[:], le[:], AX.X, ALU.add))
                            after(dve, dve_step, dve.reciprocal(lm[:], lm[:]))
                            dve.wait_ge(pr_turned, last(n, 1))
                            dve.tensor_tensor(pr[:], le[:], lm[:].unsqueeze(2).to_broadcast([P, T, NE]), ALU.mult).then_inc(pr_ready, 1)
                    dve.wait_ge(v_stored, last(n, 16))
                    for t in range(T):
                        dve.wait_ge(v_made, this(n, T, t + 1))
                        dve.tensor_tensor(vo[:, t, :, 0:HS], pQ[:, t % 2, 0:D].rearrange("p (h e) -> p h e", h=NH),
                                          bv[:].rearrange("p (h e) -> p h e", h=NH), ALU.add).then_inc(v_ready, 1)
                    dve.wait_ge(d_made, last(n, T))
                    for f in range(NF):
                        dve.wait_ge(u_made, this(n, NF, f + 1))
                        dve.wait_ge(gelu_done, this(n, NF, f + 1))
                        dve.tensor_tensor(hid[:, f], pU[:], gel[:, f % 2], ALU.mult).then_inc(hid_ready, 1)
                    dve.wait_ge(fo_stored, last(n, 16))
                    for t in range(T):
                        dve.wait_ge(d_made, this(n, T, t + 1))
                        dve.tensor_copy(fo[:, t], pQ[:, t % 2, 0:D]).then_inc(fo_ready, 1)


def choose_tokens(nc, w, score_d, idx_d, wt_d):
    B, NE, N = score_d.shape
    CAP = N * 2 // NE
    with ExitStack() as ctx:
        sb, ps, sem = _memory(nc, ctx, "b_")
        ident = sb("ident", [P, P])
        first_row = sb("first_row", [P, 1])
        cur = sb("cur", [P, 2, N])
        vals = sb("vals", [P, CAP])
        idx = sb("idx", [P, CAP], U32)
        idxf = sb("idxf", [P, CAP])
        idxo = sb("idxo", [P, P], U32)
        wto = sb("wto", [P, P])
        pI = ps("pI", [P, P])
        pW = ps("pW", [P, 512])
        loaded, step, chosen, turned, stored = sem("loaded"), sem("step"), sem("chosen"), sem("turned"), sem("stored")
        ready = sem("ready")
        block = ctx.enter_context(nc.Block())

        @block.sync
        def _(sp):
            sp.dma_start(cur[:, 0], score_d.rearrange("b e n -> (b e) n")).then_inc(loaded, 16)
            sp.dma_start(ident[:], w["ident"]).then_inc(loaded, 16)
            sp.dma_start(first_row[:], w["first_row"]).then_inc(loaded, 16)
            sp.wait_ge(ready, 2)
            sp.dma_start(idx_d, idxo[:]).then_inc(stored, 16)
            sp.dma_start(wt_d, wto[:]).then_inc(stored, 16)
            sp.wait_ge(stored, 32)

        @block.vector
        def _(dve):
            dve.wait_ge(loaded, 48)
            for r in range(CAP // 8):
                a, b, eight = cur[:, r % 2], cur[:, (r + 1) % 2], slice(8 * r, 8 * r + 8)
                after(dve, step, dve.max(vals[:, eight], a))
                dve.max_index(idx[:, eight], vals[:, eight], a)
                after(dve, step, dve.match_replace(b, vals[:, eight], a, -1.0))
            after(dve, step, dve.tensor_copy(idxf[:], idx[:]))
            dve.tensor_scalar(idxf[:], idxf[:], first_row[:, 0:1], None, ALU.add).then_inc(chosen, 1)
            dve.wait_ge(turned, 1)
            dve.tensor_copy(idxo[:], pI[:]).then_inc(ready, 1)
            dve.tensor_copy(wto[:], pW[:, 0:P]).then_inc(ready, 1)

        @block.tensor
        def _(pe):
            pe.wait_ge(chosen, 1)
            pe.transpose(pI[:], idxf[:], ident[:])
            pe.transpose(pW[:, 0:P], vals[:], ident[:]).then_inc(turned, 1)

Q_PARTS = (3, 2, 1)


def attend(nc, w, qk_d, v_d, att_d):
    B, _, _, DQ, N = qk_d.shape
    HS = 16
    HT = 4
    NG = DQ // HS // HT
    NB = N // P
    R = sum(Q_PARTS) * HS
    R2 = R + 3 * NB
    E1 = HS + 1
    G = 32
    turns = B * NG
    AHEAD = 6
    rows1 = [(q, c, min(512, (q + 1) * P - c)) for q in range(NB) for c in range(0, (q + 1) * P, 512)]
    rows2 = [(k, max(c, k * P), c + 512 - max(c, k * P)) for k in range(NB) for c in range(k * P // 512 * 512, N, 512)]
    NPC = len(rows1)
    assert len(rows2) == NPC
    base = [0]
    for k in range(NB):
        base.append(base[-1] + N - k * P)
    with ExitStack() as ctx:
        sb, ps, sem = _memory(nc, ctx, "c_")
        consts = sb("consts", [P, 3 + NB, P])
        constsb = sb("constsb", [P, 3 + NB, P], BF16)
        identb, mask1, mask2, blocks = constsb[:, 0], constsb[:, 1], constsb[:, 2], constsb[:, 3:]
        qs = sb("qs", [P, HT, N], BF16)
        ks = sb("ks", [P, HT, N], BF16)
        gather = sb("gather", [P, E1])
        vs = sb("vs", [P, 2, NB, 2, G])
        mx = sb("mx", [P, NB, 2])
        mq = sb("mq", [P, NB])
        mr = sb("mr", [P, NB])
        mp = sb("mp", [P, 3 * NB], BF16)
        pr = sb("pr", [P, 2, base[-1]])
        oT = sb("oT", [P, N])
        rec = sb("rec", [P, NB])
        on = sb("on", [P, 2, NB, 2, HS])
        p1 = ps("p1", [P, 2, 512])
        p2 = ps("p2", [P, 2, 512])
        pT = ps("pT", [P, 2, 512])
        pM = ps("pM", [P, 1024], BF16)
        pO = ps("pO", [P, 512])
        consts_ready = sem("consts_ready")
        consts_in, qk_in, v_in = sem("consts_in"), [sem(f"qk_in{j}") for j in range(HT)], [sem("v_in0"), sem("v_in1")]
        s1_made, s1_used, max_ready, max_turned, max_placed = sem("s1_made"), sem("s1_used"), sem("max_ready"), sem("max_turned"), sem("max_placed")
        s2_made, exp_done, o_made, on_ready, on_stored = sem("s2_made"), sem("exp_done"), sem("o_made"), sem("on_ready"), sem("on_stored")
        on_free = sem("on_free")
        dve_step, qs_clear = sem("dve_step"), sem("qs_clear")
        av_made, ot_ready = sem("av_made"), sem("ot_ready")
        block = ctx.enter_context(nc.Block())
        outt = att_d.rearrange("(b t p) (g h j e) -> b g h p t j e", b=B, p=P, h=2, j=2, e=HS)
        vt = v_d.rearrange("b (t p) (g h j e) -> b g h p t j e", p=P, h=2, j=2, e=E1)
        qkt = qk_d.rearrange("b s r (g j e) n -> b g j s r e n", j=HT, e=HS)

        @block.sync
        def _(sp):
            for dst, name in ((consts[:, 0], "ident"), (consts[:, 1], "mask1"), (consts[:, 2], "mask2"), (consts[:, 3:], "blocks"), (gather[:], "gather")):
                sp.dma_start(dst, w[name]).then_inc(consts_in, 16)
            sp.wait_ge(qs_clear, 1)
            with sp.Fori(0, B) as b:
                with sp.Fori(0, NG) as g:
                    m = b * NG + g
                    for j in range(HT):
                        sp.wait_ge(s2_made, last(m, HT * NPC, (j + 1) * NPC))
                        row = 0
                        for kp, parts in enumerate(Q_PARTS):
                            for dst, src in ((qs, qkt[b, g, j, 0, 0:parts]), (ks, qkt[b, g, j, 1, kp].unsqueeze(0).to_broadcast([parts, HS, N]))):
                                sp.dma_start(dst[row:row + parts * HS, j], src).then_inc(qk_in[j], 16)
                            row += parts * HS
                        if j % 2:
                            sp.wait_ge(av_made, last(m, HT, j + 1))
                            for i in range(2):
                                sp.dma_start(vs[:, j // 2, :, i, 0:E1], vt[b, g, j // 2, :, :, i]).then_inc(v_in[j // 2], 16)

        @block.gpsimd
        def _(pool):
            pool.sem_inc(on_free, 2)
            with pool.Fori(0, B) as b:
                with pool.Fori(0, NG) as g:
                    m = b * NG + g
                    for p in range(2):
                        pool.wait_ge(on_ready, this(m, HT, 2 * p + 2))
                        pool.dma_start(outt[b, g, p], on[:, p]).then_inc(on_stored, 16)
                        pool.wait_ge(on_stored, m * 32 + p * 16 + 16)
                        pool.sem_inc(on_free, 1)

        def scores1(pe, m, j, i):
            q, c, width = rows1[i]
            diagonal = c + width == (q + 1) * P
            pe.wait_ge(s1_used, this(m, HT * NPC, j * NPC + i - 1))
            out = p1[:, (j * NPC + i) % 2]
            mm = pe.matmul(out[:, 0:width], qs[0:R, j % HT, q * P:(q + 1) * P], ks[0:R, j % HT, c:c + width], start=True, stop=not diagonal)
            if diagonal:
                mm = pe.matmul(out[:, width - P:width], identb, mask1, start=False, stop=True)
            mm.then_inc(s1_made, 1)

        def scores2(pe, m, j, i):
            k, c, width = rows2[i]
            pe.wait_ge(exp_done, this(m, HT * NPC, j * NPC + i - 1))
            out = p2[:, i % 2]
            mm = pe.matmul(out[:, 0:width], ks[0:R2, j % HT, k * P:(k + 1) * P], qs[0:R2, j % HT, c:c + width], start=True, stop=c != k * P)
            if c == k * P:
                mm = pe.matmul(out[:, 0:P], identb, mask2, start=False, stop=True)
            mm.then_inc(s2_made, 1)

        def turn_maxima(pe, m, j):
            pe.wait_ge(max_ready, this(m, HT, j + 1))
            pe.wait_ge(max_placed, this(m, HT, j))
            pe.transpose(pM[R:R2, 0:P], mp[:], identb, tile_position=(0, R)).then_inc(max_turned, 1)

        @block.tensor
        def _(pe):
            for q, per in ((s1_made, NPC), (max_turned, 1), (s2_made, NPC), (av_made, 1), (o_made, 1)):
                pe.sem_inc(q, HT * per)
            pe.wait_ge(consts_ready, 1)
            pe.wait_ge(consts_in, 80)
            pe.wait_ge(qs_clear, 1)

            def weigh(m, j, i):
                k, c, width = rows2[i]
                if i == 0:
                    pe.wait_ge(v_in[j // 2], m * 32 + 32)
                    pe.wait_ge(ot_ready, this(m, HT, j))
                pe.wait_ge(exp_done, this(m, HT * NPC, j * NPC + i + 1))
                rows = slice(k % 4 * G, k % 4 * G + G)
                at = base[k] + c - k * P
                mm = pe.matmul(pT[rows, c // 512, c % 512:c % 512 + width], vs[:, j // 2, k, j % 2, :], pr[:, j % 2, at:at + width],
                               start=k < 4, stop=k >= 4 or c < 512, tile_position=(0, k % 4 * G))
                if i == NPC - 1:
                    mm.then_inc(av_made, 1)

            def outputs(m, j):
                pe.wait_ge(ot_ready, this(m, HT, j + 1))
                pe.wait_ge(on_ready, this(m, HT, j))
                for q in range(NB):
                    mm = pe.matmul(pO[:, q * E1:(q + 1) * E1], oT[:, q * P:(q + 1) * P], gather[:], start=True, stop=True)
                mm.then_inc(o_made, 1)

            def begin(m, j, more):
                if more >= 1:
                    pe.wait_ge(qk_in[j % HT], m * 96 + (96 if j < HT else 192))
                if more >= 0:
                    pe.wait_ge(max_placed, this(m, HT, j))
                for i in range(AHEAD):
                    if more >= 1:
                        scores1(pe, m, j, i)
                    if more >= 0:
                        scores2(pe, m, j - 1, i)

            def heads(m, j, more):
                for i in range(AHEAD, NPC):
                    if more >= 2:
                        scores1(pe, m, j + 2, i)
                    if more >= 1:
                        scores2(pe, m, j + 1, i)
                    weigh(m, j, i - AHEAD)
                if more >= 2:
                    turn_maxima(pe, m, j + 2)
                for i in range(NPC - AHEAD, NPC):
                    weigh(m, j, i)
                begin(m, j + 3, more - 2)
                outputs(m, j)

            pe.wait_ge(qk_in[0], 96)
            for i in range(NPC):
                scores1(pe, 0, 0, i)
            turn_maxima(pe, 0, 0)
            pe.wait_ge(qk_in[1], 96)
            pe.wait_ge(max_placed, this(0, HT, 1))
            for i in range(NPC):
                scores1(pe, 0, 1, i)
                scores2(pe, 0, 0, i)
            turn_maxima(pe, 0, 1)
            begin(0, 2, 1)
            with pe.Fori(0, turns - 1) as m:
                for j in range(HT):
                    heads(m, j, 3)
            for j in range(HT):
                heads(turns - 1, j, HT - 1 - j)

        @block.scalar
        def _(act):
            act.sem_inc(exp_done, HT * NPC)
            act.sem_inc(ot_ready, HT)

            def exponentials(m, j):
                act.wait_ge(av_made, this(m, HT, j - 1))
                for i, (k, c, width) in enumerate(rows2):
                    act.wait_ge(s2_made, this(m, HT * NPC, j * NPC + i + 1))
                    at = base[k] + c - k * P
                    act.activation(pr[:, j % 2, at:at + width], p2[:, i % 2, 0:width], AF.Exp).then_inc(exp_done, 1)

            def copy_turned(m, j):
                act.wait_ge(av_made, this(m, HT, j + 1))
                act.wait_ge(o_made, this(m, HT, j))
                act.copy(oT[:], pT[:].rearrange("p a n -> p (a n)")).then_inc(ot_ready, 1)

            exponentials(0, 0)
            with act.Fori(0, turns - 1) as m:
                for j in range(HT):
                    exponentials(m, j + 1)
                    copy_turned(m, j)
            for j in range(HT):
                if j < HT - 1:
                    exponentials(turns - 1, j + 1)
                copy_turned(turns - 1, j)

        def piece_maxima(dve, m, j, pieces):
            for i in pieces:
                q, c, width = rows1[i]
                dve.wait_ge(s1_made, this(m, HT * NPC, j * NPC + i + 1))
                dve.tensor_reduce(mx[:, q, c // 512:c // 512 + 1], p1[:, (j * NPC + i) % 2, 0:width], AX.X, ALU.max).then_inc(s1_used, 1)

        def place_maxima(dve, m, j):
            dve.wait_ge(s1_used, this(m, HT * NPC, (j + 1) * NPC))
            after(dve, dve_step, dve.tensor_reduce(mq[:], mx[:], AX.X, ALU.max))
            dve.wait_ge(max_turned, this(m, HT, j))
            after(dve, dve_step, dve.tensor_scalar(mp[:, 0:NB], mq[:], -1.0, None, ALU.mult))
            after(dve, dve_step, dve.scalar_tensor_tensor(mr[:], mq[:], -1.0, mp[:, 0:NB], ALU.mult, ALU.subtract))
            after(dve, dve_step, dve.tensor_copy(mp[:, NB:2 * NB], mr[:]))
            dve.tensor_tensor(mp[:, 2 * NB:], mr[:], mp[:, NB:2 * NB], ALU.subtract).then_inc(max_ready, 1)
            dve.wait_ge(max_turned, this(m, HT, j + 1))
            dve.wait_ge(s2_made, this(m, HT * NPC, (j - HT + 1) * NPC))
            dve.tensor_tensor(qs[R:R2, j % HT].rearrange("p (t q) -> p t q", t=NB),
                              pM[R:R2, 0:P].unsqueeze(1).to_broadcast([3 * NB, NB, P]), blocks[R:R2], ALU.mult).then_inc(max_placed, 1)

        def finish(dve, m, j):
            dve.wait_ge(o_made, this(m, HT, j + 1))
            o = pO[:, 0:NB * E1].rearrange("p (t e) -> p t e", e=E1)
            after(dve, dve_step, dve.reciprocal(rec[:], o[:, :, HS]))
            dve.wait_ge(on_free, m * 2 + j // 2 + 1)
            dve.tensor_tensor(on[:, j // 2, :, j % 2], o[:, :, 0:HS], rec[:].unsqueeze(2).to_broadcast([P, NB, HS]), ALU.mult).then_inc(on_ready, 1)

        @block.vector
        def _(dve):
            for q, per in ((s1_used, NPC), (max_ready, 1), (max_placed, 1), (on_ready, 1)):
                dve.sem_inc(q, HT * per)
            dve.memset(ks[R:P], 1.0)
            dve.memset(vs[:], 0.0)
            dve.memset(pT[:], 0.0)
            dve.memset(mx[:], -3e38).then_inc(qs_clear, 1)
            dve.wait_ge(qs_clear, 1)
            dve.wait_ge(consts_in, 80)
            dve.tensor_copy(constsb[:], consts[:]).then_inc(consts_ready, 1)
            dve.wait_ge(consts_ready, 1)
            for j in range(2):
                piece_maxima(dve, 0, j, range(NPC))
                place_maxima(dve, 0, j)
            piece_maxima(dve, 0, 2, range(AHEAD))

            def heads(m, j, more):
                if more >= 2:
                    piece_maxima(dve, m, j + 2, range(AHEAD, NPC))
                    place_maxima(dve, m, j + 2)
                if more >= 3:
                    piece_maxima(dve, m, j + 3, range(AHEAD))
                finish(dve, m, j)

            with dve.Fori(0, turns - 1) as m:
                for j in range(HT):
                    heads(m, j, 3)
            for j in range(HT):
                heads(turns - 1, j, HT - 1 - j)


def run_experts(nc, w, xn_d, idx_d, wt_d, ffn_d):
    D = xn_d.shape[1]
    NE, B = 16, 8
    T = B // 2
    C = T * P
    K2 = D // P
    NF = 4
    turns = 2 * NE
    with ExitStack() as ctx:
        sb, ps, sem = _memory(nc, ctx, "e_")
        ident = sb("ident", [P, P])
        idx = sb("idx", [P, B, NE], U32)
        wt = sb("wt", [P, B, NE])
        idx_e = sb("idx_e", [P, 2, T], U32)
        wt_e = sb("wt_e", [P, T])
        wg = sb("wg", [P, 2, K2, NF, P])
        wu = sb("wu", [P, 2, K2, NF, P])
        wd = sb("wd", [P, 2, NF, D])
        xg = sb("xg", [P, 2, T, D])
        xT = sb("xT", [P, K2, C])
        gel = sb("gel", [P, 2, C])
        hid = sb("hid", [P, NF, C])
        eo = sb("eo", [P, 2, T, D])
        pT = ps("pT", [P, K2, C])
        pG = ps("pG", [P, 2, C])
        pU = ps("pU", [P, 2, C])
        pD = ps("pD", [P, 2, 512])
        consts_in, w_in, gathered = sem("consts_in"), [sem("w_in0"), sem("w_in1")], [sem("gathered0"), sem("gathered1")]
        idx_staged, wt_staged, added = sem("idx_staged"), sem("wt_staged"), sem("added")
        add_begun, add_ended = sem("add_begun"), sem("add_ended")
        turned, xT_ready, g_made, u_made, gelu_done, hid_ready, d_made, eo_ready = (
            sem("turned"), sem("xT_ready"), sem("g_made"), sem("u_made"), sem("gelu_done"), sem("hid_ready"), sem("d_made"), sem("eo_ready"))
        block = ctx.enter_context(nc.Block())
        pairs = [(ep, g, ep * 2 + g) for ep in range(2) for g in range(2)]

        @block.sync
        def _(sp):
            for dst, src in ((ident[:], w["ident"]), (idx[:], idx_d.rearrange("p (b e) -> p b e", e=NE)),
                             (wt[:], wt_d.rearrange("p (b e) -> p b e", e=NE))):
                sp.dma_start(dst, src).then_inc(consts_in, 16)
            with sp.Fori(0, NE // 2) as e2:
                for ep in range(2):
                    sp.wait_ge(d_made, last(e2, 4 * T, (ep + 1) * 2 * T))
                    for dst, name in ((wg, "Wg"), (wu, "Wu"), (wd, "Wd")):
                        sp.dma_start(dst[:, ep], w[name][e2 * 2 + ep]).then_inc(w_in[ep], 16)

        def gather(pool, e, g, turn_after):
            pool.wait_ge(turned, turn_after)
            pool.tensor_copy(idx_e[:, g], idx[:, g * T:(g + 1) * T, e]).then_inc(idx_staged, 1)
            pool.wait_ge(idx_staged, 1)
            pool.sem_inc(idx_staged, -1)
            for t in range(T):
                pool.indirect_dma_start(out=xg[:, g, t], out_offset=None, in_=xn_d,
                                        in_offset=bass.IndirectOffsetOnAxis(ap=idx_e[:, g, t:t + 1], axis=0)).then_inc(gathered[g], 16)

        def pool_pair(pool, e2, ends):
            for ep, g, m in pairs:
                n = e2 * 4 + m
                pool.wait_ge(eo_ready, this(n, T))
                pool.sem_inc(add_begun, 1)
                for t in range(T):
                    pool.indirect_dma_start(out=ffn_d, out_offset=bass.IndirectOffsetOnAxis(ap=idx_e[:, g, t:t + 1], axis=0),
                                            in_=eo[:, g, t], in_offset=None, compute_op=ALU.add).then_inc(added, 16)
                pool.wait_ge(added, (n + 1) * 16 * T)
                pool.sem_inc(add_ended, 1)
                if not (ends and ep == 1):
                    gather(pool, e2 * 2 + ep + 1, g, this(n, 1))

        @block.gpsimd
        def _(pool):
            pool.sem_inc(add_ended, 1)
            pool.wait_ge(consts_in, 48)
            for g in range(2):
                gather(pool, 0, g, 1)
            with pool.Fori(0, NE // 2 - 1) as e2:
                pool_pair(pool, e2, False)
            pool_pair(pool, NE // 2 - 1, True)

        @block.tensor
        def _(pe):
            for q, per in ((turned, 1), (g_made, NF), (u_made, NF), (d_made, 4 * T)):
                pe.sem_inc(q, per)
            pe.wait_ge(consts_in, 48)
            with pe.Fori(0, NE // 2) as e2:
                for ep, g, m in pairs:
                    n = e2 * 4 + m
                    pe.wait_ge(gathered[g], (e2 * 2 + ep + 1) * 16 * T)
                    for k in range(K2):
                        for t in range(T):
                            mm = pe.transpose(pT[:, k, t * P:(t + 1) * P], xg[:, g, t, k * P:(k + 1) * P], ident[:])
                    mm.then_inc(turned, 1)
                    if g == 0:
                        pe.wait_ge(w_in[ep], e2 * 48 + 48)
                    pe.wait_ge(xT_ready, this(n, 1))
                    for f in range(NF):
                        pe.wait_ge(gelu_done, this(n, NF, f - 1))
                        for k in range(K2):
                            mm = pe.matmul(pG[:, f % 2], wg[:, ep, k, f, :], xT[:, k, :], start=k == 0, stop=k == K2 - 1)
                        mm.then_inc(g_made, 1)
                        pe.wait_ge(hid_ready, this(n, NF, f - 1))
                        for k in range(K2):
                            mm = pe.matmul(pU[:, f % 2], wu[:, ep, k, f, :], xT[:, k, :], start=k == 0, stop=k == K2 - 1)
                        mm.then_inc(u_made, 1)
                    pe.wait_ge(hid_ready, this(n, NF))
                    for t in range(T):
                        pe.wait_ge(eo_ready, this(n, T, t - 1))
                        for f in range(NF):
                            mm = pe.matmul(pD[:, t % 2, 0:D], hid[:, f, t * P:(t + 1) * P], wd[:, ep, f, :], start=f == 0, stop=f == NF - 1)
                        mm.then_inc(d_made, 1)

        @block.scalar
        def _(act):
            act.sem_inc(xT_ready, 1)
            act.sem_inc(gelu_done, NF)
            with act.Fori(0, turns) as n:
                act.wait_ge(turned, this(n, 1))
                act.wait_ge(u_made, last(n, NF))
                for k in range(K2):
                    cp = act.copy(xT[:, k], pT[:, k])
                cp.then_inc(xT_ready, 1)
                for f in range(NF):
                    act.wait_ge(g_made, this(n, NF, f + 1))
                    act.wait_ge(hid_ready, this(n, NF, f - 1))
                    act.activation(gel[:, f % 2], pG[:, f % 2], AF.Gelu).then_inc(gelu_done, 1)

        @block.vector
        def _(dve):
            for q, per in ((wt_staged, 1), (hid_ready, NF), (eo_ready, T)):
                dve.sem_inc(q, per)
            dve.wait_ge(consts_in, 48)
            with dve.Fori(0, NE) as e:
                for g in range(2):
                    n = e * 2 + g
                    dve.wait_ge(eo_ready, last(n, T))
                    dve.tensor_copy(wt_e[:], wt[:, g * T:(g + 1) * T, e]).then_inc(wt_staged, 1)
                    dve.wait_ge(d_made, last(n, T) + 3 * T)
                    for f in range(NF):
                        dve.wait_ge(u_made, this(n, NF, f + 1))
                        dve.wait_ge(gelu_done, this(n, NF, f + 1))
                        dve.tensor_tensor(hid[:, f], pU[:, f % 2], gel[:, f % 2], ALU.mult).then_inc(hid_ready, 1)
                    dve.wait_ge(wt_staged, this(n, 1))
                    dve.wait_ge(add_ended, last(n, 1))
                    for t in range(T):
                        dve.wait_ge(d_made, this(n, T, t + 1) + 3 * T)
                        dve.tensor_scalar(eo[:, g, t], pD[:, t % 2, 0:D], wt_e[:, t:t + 1], None, ALU.mult).then_inc(eo_ready, 1)


def finish_l0(nc, x, w, att_d, ffn_d, x1_d, xnT_d, gate_d):
    B, N, D = x.shape
    C = 512
    T = C // P
    K2 = D // P
    NE, M, MS = 16, 10, 2
    with ExitStack() as ctx:
        sb, ps, sem = _memory(nc, ctx, "f_")
        ident = sb("ident", [P, P])
        wo = sb("wo", [P, K2, D])
        bo = sb("bo", [P, D])
        wr = sb("wr", [P, K2, NE])
        wg = sb("wg", [P, K2, M, P])
        wu = sb("wu", [P, K2, M, P])
        wd = sb("wd", [P, M, D])
        spread = sb("spread", [NE, M - MS, P])
        iota = sb("iota", [P, NE])
        minus_half = sb("minus_half", [P, T])
        xin = sb("xin", [P, 2, T, D])
        att = sb("att", [P, 2, T, D])
        ffn = sb("ffn", [P, 2, T, D])
        aT = sb("aT", [P, K2, C])
        x1 = sb("x1", [P, T, D])
        stats = sb("stats", [P, T, 6])
        mv = sb("mv", [P, T, 2])
        veps = sb("veps", [P, T])
        rstd = sb("rstd", [P, T])
        xn = sb("xn", [P, T, D])
        xnT = sb("xnT", [P, K2, C])
        lg = sb("lg", [P, T, NE])
        le = sb("le", [P, T, NE])
        lm = sb("lm", [P, T])
        top = sb("top", [P, T, 8])
        topi = sb("topi", [P, T, 8], U32)
        topf = sb("topf", [P, T, 8])
        c1 = sb("c1", [P, T, NE])
        c2 = sb("c2", [P, T, NE])
        cT = sb("cT", [NE, C])
        sil = sb("sil", [P, 2, C])
        hid = sb("hid", [P, M, C])
        go = sb("go", [P, T, D])
        pT = ps("pT", [P, K2, C])
        pA = ps("pA", [P, 2, 512])
        pG = ps("pG", [P, C])
        pU = ps("pU", [P, C])
        pC = ps("pC", [P, C])
        pL = ps("pL", [P, C])

        weights_in, tokens_in = sem("weights_in"), [sem("tokens_in0"), sem("tokens_in1")]
        dve_step, pool_step = sem("dve_step"), sem("pool_step")
        att_turned, aT_ready, o_made, silu_ready, x1_ready, x1_stored = (
            sem("att_turned"), sem("aT_ready"), sem("o_made"), sem("silu_ready"), sem("x1_ready"), sem("x1_stored"))
        o_used = sem("o_used")
        var_ready, rstd_ready, xn_ready, xn_turned, xnT_ready, xnT_stored = (
            sem("var_ready"), sem("rstd_ready"), sem("xn_ready"), sem("xn_turned"), sem("xnT_ready"), sem("xnT_stored"))
        l_made, l_shifted, l_exp, c_ready, c_turned, cT_ready = (
            sem("l_made"), sem("l_shifted"), sem("l_exp"), sem("c_ready"), sem("c_turned"), sem("cT_ready"))
        g_made, u_made, c_made, silu_done, hid_ready, c_used = (
            sem("g_made"), sem("u_made"), sem("c_made"), sem("silu_done"), sem("hid_ready"), sem("c_used"))
        d_made, go_ready, go_stored = sem("d_made"), sem("go_ready"), sem("go_stored")
        block = ctx.enter_context(nc.Block())

        def tiles(a):
            return a.rearrange("(b c t p) d -> b c p t d", b=B, c=2, p=P)

        xt = x.rearrange("b (c t p) d -> b c p t d", c=2, p=P)
        attt, ft, x1t, gt = tiles(att_d), tiles(ffn_d), tiles(x1_d), tiles(gate_d)
        xnTt = xnT_d.rearrange("(k p) (b c n) -> b c p k n", p=P, b=B, c=2)
        consts = ((ident, "ident"), (wo, "wo"), (bo, "bo"), (wr, "wr1"), (wg, "wg1"), (wu, "wu1"), (wd, "wd1"),
                  (spread, "spread"), (iota, "iota"))
        turn_list = range(2)

        @block.sync
        def _(sp):
            for q, per in ((x1_stored, 16), (xnT_stored, 16), (go_stored, 16)):
                sp.sem_inc(q, per)
            for dst, name in consts:
                sp.dma_start(dst[:], w[name]).then_inc(weights_in, 16)
            with sp.Fori(0, B) as b:
                for s in turn_list:
                    n = b * 2 + s
                    sp.wait_ge(x1_ready, this(n, 1))
                    sp.dma_start(x1t[b, s], x1[:]).then_inc(x1_stored, 16)
                    sp.wait_ge(xnT_ready, this(n, 1))
                    sp.dma_start(xnTt[b, s], xnT[:]).then_inc(xnT_stored, 16)
                    sp.wait_ge(go_ready, this(n, T))
                    sp.dma_start(gt[b, s], go[:]).then_inc(go_stored, 16)
            sp.wait_ge(x1_stored, this(2 * B - 1, 16))
            sp.wait_ge(xnT_stored, this(2 * B - 1, 16))
            sp.wait_ge(go_stored, this(2 * B - 1, 16))

        @block.gpsimd
        def _(pool):
            pool.sem_inc(rstd_ready, 1)
            after(pool, pool_step, pool.memset(minus_half[:], -0.5))
            with pool.Fori(0, B) as b:
                for s in turn_list:
                    n = b * 2 + s
                    pool.wait_ge(x1_ready, last(n, 1))
                    pool.dma_start(xin[:, s], xt[b, s]).then_inc(tokens_in[s], 16)
                    pool.dma_start(att[:, s], attt[b, s]).then_inc(tokens_in[s], 16)
                    pool.dma_start(ffn[:, s], ft[b, s]).then_inc(tokens_in[s], 16)
                    pool.wait_ge(var_ready, this(n, 1))
                    pool.tensor_tensor(rstd[:], veps[:], minus_half[:], ALU.pow).then_inc(rstd_ready, 1)

        @block.tensor
        def _(pe):
            for q, per in ((att_turned, 1), (o_made, T), (xn_turned, 1), (l_made, 1), (c_turned, 1), (g_made, M), (u_made, M),
                           (c_made, M - MS), (d_made, T)):
                pe.sem_inc(q, per)
            pe.wait_ge(weights_in, 16 * len(consts))
            with pe.Fori(0, B) as b:
                for s in turn_list:
                    n = b * 2 + s
                    pe.wait_ge(tokens_in[s], b * 48 + 48)
                    pe.wait_ge(xnT_ready, last(n, 1))
                    for k in range(K2):
                        for t in range(T):
                            mm = pe.transpose(pT[:, k, t * P:(t + 1) * P], att[:, s, t, k * P:(k + 1) * P], ident[:])
                    mm.then_inc(att_turned, 1)
                    pe.wait_ge(aT_ready, this(n, 1))
                    for t in range(T):
                        pe.wait_ge(*((go_ready, last(n, T, T - 1 + t)) if t < 2 else (o_used, this(n, T, t - 1))))
                        for k in range(K2):
                            mm = pe.matmul(pA[:, t % 2, 0:D], aT[:, k, t * P:(t + 1) * P], wo[:, k, :], start=k == 0, stop=k == K2 - 1)
                        mm.then_inc(o_made, 1)
                    pe.wait_ge(xn_ready, this(n, 1))
                    for k in range(K2):
                        for t in range(T):
                            mm = pe.transpose(pT[:, k, t * P:(t + 1) * P], xn[:, t, k * P:(k + 1) * P], ident[:])
                    mm.then_inc(xn_turned, 1)
                    pe.wait_ge(xnT_ready, this(n, 1))
                    pe.wait_ge(cT_ready, last(n, 1))
                    for t in range(T):
                        for k in range(K2):
                            mm = pe.matmul(pL[:, t * NE:(t + 1) * NE], xnT[:, k, t * P:(t + 1) * P], wr[:, k, :],
                                           start=k == 0, stop=k == K2 - 1)
                    mm.then_inc(l_made, 1)
                    for m in range(M):
                        if m == MS:
                            pe.wait_ge(c_ready, this(n, 1))
                            for t in range(T):
                                mm = pe.transpose(pL[0:NE, t * P:(t + 1) * P], c1[:, t, :], ident[:])
                            mm.then_inc(c_turned, 1)
                            pe.wait_ge(cT_ready, this(n, 1))
                        pe.wait_ge(silu_done, this(n, M, m))
                        for k in range(K2):
                            mm = pe.matmul(pG[:], wg[:, k, m, :], xnT[:, k, :], start=k == 0, stop=k == K2 - 1)
                        mm.then_inc(g_made, 1)
                        pe.wait_ge(hid_ready, this(n, M, m))
                        for k in range(K2):
                            mm = pe.matmul(pU[:], wu[:, k, m, :], xnT[:, k, :], start=k == 0, stop=k == K2 - 1)
                        mm.then_inc(u_made, 1)
                        if m >= MS:
                            pe.wait_ge(c_used, this(n, M - MS, m - MS))
                            pe.matmul(pC[:], spread[:, m - MS, :], cT[:], start=True, stop=True).then_inc(c_made, 1)
                    pe.wait_ge(c_used, this(n, M - MS))
                    for t in range(T):
                        pe.wait_ge(*((o_used, this(n, T, T - 1 + t)) if t < 2 else (go_ready, this(n, T, t - 1))))
                        for m in range(M):
                            mm = pe.matmul(pA[:, t % 2, 0:D], hid[:, m, t * P:(t + 1) * P], wd[:, m, :], start=m == 0, stop=m == M - 1)
                        mm.then_inc(d_made, 1)

        @block.scalar
        def _(act):
            for q, per in ((aT_ready, 1), (silu_ready, 1), (xnT_ready, 1), (l_exp, 1), (cT_ready, 1), (silu_done, M), (go_ready, T)):
                act.sem_inc(q, per)
            with act.Fori(0, B) as b:
                for s in turn_list:
                    n = b * 2 + s
                    act.wait_ge(tokens_in[s], b * 48 + 48)
                    act.activation(ffn[:, s], ffn[:, s], AF.Silu).then_inc(silu_ready, 1)
                    act.wait_ge(att_turned, this(n, 1))
                    act.wait_ge(o_made, last(n, T))
                    for k in range(K2):
                        cp = act.copy(aT[:, k], pT[:, k])
                    cp.then_inc(aT_ready, 1)
                    act.wait_ge(xn_turned, this(n, 1))
                    act.wait_ge(u_made, last(n, M))
                    act.wait_ge(xnT_stored, last(n, 16))
                    for k in range(K2):
                        cp = act.copy(xnT[:, k], pT[:, k])
                    cp.then_inc(xnT_ready, 1)
                    act.wait_ge(l_shifted, this(n, 1))
                    act.activation(le[:], lg[:], AF.Exp).then_inc(l_exp, 1)
                    for m in range(M):
                        if m == MS:
                            act.wait_ge(c_turned, this(n, 1))
                            act.copy(cT[:], pL[0:NE, :]).then_inc(cT_ready, 1)
                        act.wait_ge(g_made, this(n, M, m + 1))
                        act.wait_ge(hid_ready, this(n, M, m - 1))
                        act.activation(sil[:, m % 2], pG[:], AF.Silu).then_inc(silu_done, 1)
                    act.wait_ge(go_stored, last(n, 16))
                    for t in range(T):
                        act.wait_ge(d_made, this(n, T, t + 1))
                        act.activation(go[:, t], pA[:, t % 2, 0:D], AF.Silu).then_inc(go_ready, 1)

        @block.vector
        def _(dve):
            for q, per in ((o_used, T), (x1_ready, 1), (var_ready, 1), (xn_ready, 1), (l_shifted, 1), (c_ready, 1), (hid_ready, M),
                           (c_used, M - MS)):
                dve.sem_inc(q, per)
            dve.wait_ge(weights_in, 16 * len(consts))
            with dve.Fori(0, B) as b:
                for s in turn_list:
                    n = b * 2 + s
                    dve.wait_ge(x1_stored, last(n, 16))
                    dve.wait_ge(xn_ready, last(n, 1))
                    for t in range(T):
                        dve.wait_ge(o_made, this(n, T, t + 1))
                        dve.tensor_tensor(x1[:, t], pA[:, t % 2, 0:D], bo[:], ALU.add).then_inc(o_used, 1)
                    dve.wait_ge(o_used, this(n, T))
                    dve.wait_ge(silu_ready, this(n, 1))
                    after(dve, dve_step, dve.tensor_tensor(x1[:], x1[:], ffn[:, s], ALU.mult))
                    dve.tensor_tensor(x1[:], x1[:], xin[:, s], ALU.add).then_inc(x1_ready, 1)
                    dve.wait_ge(x1_ready, this(n, 1))
                    for t in range(T):
                        st = dve.bn_stats(stats[:, t], x1[:, t])
                    after(dve, dve_step, st)
                    for t in range(T):
                        st = dve.bn_aggr(mv[:, t], stats[:, t])
                    after(dve, dve_step, st)
                    dve.tensor_scalar_add(veps[:], mv[:, :, 1], 1e-5).then_inc(var_ready, 1)
                    dve.wait_ge(rstd_ready, this(n, 1))
                    dve.wait_ge(xn_turned, last(n, 1))
                    for t in range(T):
                        st = dve.tensor_scalar(xn[:, t], x1[:, t], mv[:, t, 0:1], rstd[:, t:t + 1], ALU.subtract, ALU.mult)
                    st.then_inc(xn_ready, 1)
                    dve.wait_ge(l_made, this(n, 1))
                    pl = pL[:, 0:T * NE].rearrange("p (t e) -> p t e", t=T)
                    wide = [P, T, NE]
                    after(dve, dve_step, dve.tensor_reduce(lm[:], pl, AX.X, ALU.max))
                    dve.tensor_tensor(lg[:], pl, lm[:].unsqueeze(2).to_broadcast(wide), ALU.subtract).then_inc(l_shifted, 1)
                    dve.wait_ge(l_exp, this(n, 1))
                    after(dve, dve_step, dve.tensor_reduce(lm[:], le[:], AX.X, ALU.add))
                    after(dve, dve_step, dve.reciprocal(lm[:], lm[:]))
                    after(dve, dve_step, dve.tensor_tensor(lg[:], le[:], lm[:].unsqueeze(2).to_broadcast(wide), ALU.mult))
                    for t in range(T):
                        mx = dve.max(top[:, t], lg[:, t])
                    after(dve, dve_step, mx)
                    for t in range(T):
                        mx = dve.max_index(topi[:, t], top[:, t], lg[:, t])
                    after(dve, dve_step, mx)
                    dve.tensor_copy(topf[:], topi[:])
                    after(dve, dve_step, dve.tensor_tensor(lm[:], top[:, :, 0], top[:, :, 1], ALU.add))
                    after(dve, dve_step, dve.tensor_scalar_add(lm[:], lm[:], 1e-9))
                    after(dve, dve_step, dve.reciprocal(lm[:], lm[:]))
                    after(dve, dve_step, dve.tensor_tensor(top[:, :, 0:2], top[:, :, 0:2], lm[:].unsqueeze(2).to_broadcast([P, T, 2]), ALU.mult))
                    dve.wait_ge(c_turned, last(n, 1))
                    for t in range(T):
                        dve.tensor_scalar(c1[:, t], iota[:], topf[:, t, 0:1], top[:, t, 0:1], ALU.is_equal, ALU.mult)
                        cc = dve.tensor_scalar(c2[:, t], iota[:], topf[:, t, 1:2], top[:, t, 1:2], ALU.is_equal, ALU.mult)
                    after(dve, dve_step, cc)
                    dve.tensor_tensor(c1[:], c1[:], c2[:], ALU.add).then_inc(c_ready, 1)
                    dve.wait_ge(d_made, last(n, T))
                    for m in range(M):
                        dve.wait_ge(u_made, this(n, M, m + 1))
                        dve.wait_ge(silu_done, this(n, M, m + 1))
                        dve.tensor_tensor(hid[:, m], pU[:], sil[:, m % 2], ALU.mult).then_inc(hid_ready, 1)
                        if m >= MS:
                            dve.wait_ge(hid_ready, this(n, M, m + 1))
                            dve.wait_ge(c_made, this(n, M - MS, m - MS + 1))
                            dve.tensor_tensor(hid[:, m], pC[:], hid[:, m], ALU.mult).then_inc(c_used, 1)


def project_l1(nc, w, xnT_d, kq_d, v_d, silu_gate_d, nsq_d, ab_d):
    B, H, C = 8, 8, 512
    D = xnT_d.shape[0]
    T, K2 = C // P, D // P
    M, MV = 20, 4
    MQK = M - MV
    with ExitStack() as ctx:
        sb, ps, sem = _memory(nc, ctx, "g_")
        ident = sb("ident", [P, P])
        wp = sb("wp", [P, K2, M, P])
        taps = sb("taps", [P, M, 4])
        wgate = sb("wgate", [P, K2, 512])
        wab = sb("wab", [P, K2, 2 * H])
        norm_w = sb("norm_w", [P, 512])
        ones = sb("ones", [P, 1])
        xT = sb("xT", [P, 2, K2, C])
        raw = sb("raw", [P, 4, C + 4])
        tail = sb("tail", [P, M, 4])
        y = sb("y", [P, 4, C])
        z = sb("z", [P, 4, C])
        sq = sb("sq", [P, 2, C])
        vn = sb("vn", [P, T, C])
        gate = sb("gate", [P, 2, 512])
        gate_w = sb("gate_w", [P, T, 512])
        nsq = sb("nsq", [P, T, MQK])
        ab = sb("ab", [P, T, 2 * H])
        pP = ps("pP", [P, 2, C])
        pV = ps("pV", [P, C])
        pG = ps("pG", [P, 2, 512])
        pN = ps("pN", [P, 512])
        pAB = ps("pAB", [P, 512])
        weights_in, x_in = sem("weights_in"), [sem("x_in0"), sem("x_in1")]
        p_made, p_copied, conv_done, z_ready, z_stored = sem("p_made"), sem("p_copied"), sem("conv_done"), sem("z_ready"), [sem(f"z_stored{i}") for i in range(4)]
        squared, summed, nsq_ready, nsq_stored = sem("squared"), sem("summed"), sem("nsq_ready"), sem("nsq_stored")
        v_turned, v_copied, v_stored = sem("v_turned"), sem("v_copied"), sem("v_stored")
        g_made, g_silu, g_ready, g_stored = sem("g_made"), sem("g_silu"), sem("g_ready"), sem("g_stored")
        ab_made, ab_ready, ab_stored = sem("ab_made"), sem("ab_ready"), sem("ab_stored")
        tile_step, ones_set = [sem("tile_step0"), sem("tile_step1")], sem("ones_set")
        block = ctx.enter_context(nc.Block())
        xt = xnT_d.rearrange("(k p) (b c n) -> b c p k n", p=P, b=B, c=2)
        kqt = kq_d.rearrange("(b c t) p h s n -> b c s h p t n", b=B, c=2)

        def tiles(a):
            return a.rearrange("(b c t p) d -> b c p t d", b=B, c=2, p=P)

        vt, gt, nt, abt = tiles(v_d), tiles(silu_gate_d), tiles(nsq_d), tiles(ab_d)
        consts = ((ident, "ident"), (wp, "wp"), (taps, "taps"), (wgate, "wgate"), (wab, "wab"), (norm_w, "norm_w"))
        order = [(sel, h) for h in range(H) for sel in range(2)]
        USES = MQK // 4
        gate_after = {4 * t + 4: t for t in range(T)}

        @block.sync
        def _(sp):
            for q, per in ((nsq_stored, 16), (v_stored, 16), (g_stored, 16), (ab_stored, 16),
                           *((z, 16 * USES) for z in z_stored)):
                sp.sem_inc(q, per)
            for dst, name in consts:
                sp.dma_start(dst[:], w[name]).then_inc(weights_in, 16)
            with sp.Fori(0, B) as b:
                for s in range(2):
                    n = b * 2 + s
                    for m, (sel, h) in enumerate(order):
                        sp.wait_ge(z_ready, this(n, M, m + 1))
                        sp.dma_start(kqt[b, s, sel, h], z[:, m % 4].rearrange("p (t n) -> p t n", t=T)).then_inc(z_stored[m % 4], 16)
                    sp.wait_ge(nsq_ready, this(n, 1))
                    sp.dma_start(nt[b, s], nsq[:]).then_inc(nsq_stored, 16)
                    sp.wait_ge(v_copied, this(n, MV))
                    sp.dma_start(vt[b, s], vn[:]).then_inc(v_stored, 16)
                    sp.wait_ge(ab_ready, this(n, 1))
                    sp.dma_start(abt[b, s], ab[:]).then_inc(ab_stored, 16)
                    sp.wait_ge(g_ready, this(n, T))
                    sp.dma_start(gt[b, s], gate_w[:]).then_inc(g_stored, 16)
            end = 2 * B - 1
            for q, per in ((nsq_stored, 16), (v_stored, 16), (g_stored, 16), (ab_stored, 16),
                           *((z, 16 * USES) for z in z_stored)):
                sp.wait_ge(q, this(end, per))

        @block.gpsimd
        def _(pool):
            pool.sem_inc(squared, MQK)
            with pool.Fori(0, B) as b:
                for s in range(2):
                    n = b * 2 + s
                    pool.wait_ge(g_made, last(n, T))
                    pool.dma_start(xT[:, s], xt[b, s]).then_inc(x_in[s], 16)
                    for m in range(MQK):
                        pool.wait_ge(z_ready, this(n, M, m + 1))
                        pool.wait_ge(summed, this(n, MQK, m - 1))
                        pool.tensor_tensor(sq[:, m % 2], z[:, m % 4], z[:, m % 4], ALU.mult).then_inc(squared, 1)

        @block.tensor
        def _(pe):
            for q, per in ((p_made, M), (summed, MQK), (v_turned, MV), (g_made, T), (ab_made, 1)):
                pe.sem_inc(q, per)

            def sums(pe, n, m):
                pe.wait_ge(squared, this(n, MQK, m + 1))
                if m == 0:
                    pe.wait_ge(nsq_ready, last(n, 1))
                for t in range(T):
                    mm = pe.matmul(pN[:, t * MQK + m:t * MQK + m + 1], sq[:, m % 2, t * P:(t + 1) * P], ones[:], start=True, stop=True)
                mm.then_inc(summed, 1)

            def turn_v(pe, n, v):
                pe.wait_ge(z_ready, this(n, M, MQK + v + 1))
                pe.wait_ge(v_copied, this(n, MV, v))
                for t in range(T):
                    mm = pe.transpose(pV[:, t * P:(t + 1) * P], z[:, v, t * P:(t + 1) * P], ident[:])
                mm.then_inc(v_turned, 1)

            pe.wait_ge(weights_in, 16 * len(consts))
            pe.wait_ge(ones_set, 1)
            with pe.Fori(0, B) as b:
                for s in range(2):
                    n = b * 2 + s
                    pe.wait_ge(x_in[s], b * 16 + 16)
                    for m in range(M):
                        pe.wait_ge(p_copied, this(n, M, m - 1))
                        for k in range(K2):
                            mm = pe.matmul(pP[:, m % 2], wp[:, k, m, :], xT[:, s, k, :], start=k == 0, stop=k == K2 - 1)
                        mm.then_inc(p_made, 1)
                        if 4 <= m < MQK + 4:
                            sums(pe, n, m - 4)
                        if m == 2:
                            pe.wait_ge(ab_ready, last(n, 1))
                            for t in range(T):
                                for k in range(K2):
                                    mm = pe.matmul(pAB[:, t * 16:(t + 1) * 16], xT[:, s, k, t * P:(t + 1) * P], wab[:, k, :], start=k == 0, stop=k == K2 - 1)
                            mm.then_inc(ab_made, 1)
                        if m in gate_after:
                            t = gate_after[m]
                            pe.wait_ge(g_silu, this(n, T, t - 1))
                            for k in range(K2):
                                mm = pe.matmul(pG[:, t % 2], xT[:, s, k, t * P:(t + 1) * P], wgate[:, k, :], start=k == 0, stop=k == K2 - 1)
                            mm.then_inc(g_made, 1)
                    for v in range(MV):
                        turn_v(pe, n, v)

        @block.scalar
        def _(act):
            for q, per in ((p_copied, M), (z_ready, M), (v_copied, MV), (g_silu, T), (ab_ready, 1), (nsq_ready, 1)):
                act.sem_inc(q, per)

            def silu(act, n, m):
                act.wait_ge(conv_done, this(n, M, m + 1))
                if m < 4:
                    act.wait_ge(v_turned, last(n, MV, m + 1))
                else:
                    act.wait_ge(z_stored[m % 4], this(n, 16 * USES, 16 * (m // 4)))
                    act.wait_ge(squared, this(n, MQK, m - 3))
                act.activation(z[:, m % 4], y[:, m % 4], AF.Silu).then_inc(z_ready, 1)

            def copy_v(act, n, v):
                if v == 0:
                    act.wait_ge(v_stored, last(n, 16))
                act.wait_ge(v_turned, this(n, MV, v + 1))
                act.copy(vn[:, :, v * P:(v + 1) * P], pV[:].rearrange("p (t c) -> p t c", t=T)).then_inc(v_copied, 1)

            act.wait_ge(weights_in, 16 * len(consts))
            with act.Fori(0, B) as b:
                for s in range(2):
                    n = b * 2 + s
                    for m in range(M + 3):
                        if m < M:
                            act.wait_ge(p_made, this(n, M, m + 1))
                            act.wait_ge(conv_done, this(n, M, m - 3))
                            act.copy(raw[:, m % 4, 3:C + 3], pP[:, m % 2])
                            act.wait_ge(z_ready, this(n, M, m - 3))
                            act.activation(y[:, m % 4], pP[:, m % 2], AF.Copy, scale=taps[:, m, 3:4]).then_inc(p_copied, 1)
                        if m >= 3:
                            silu(act, n, m - 3)
                        if m == 5:
                            act.wait_ge(ab_stored, last(n, 16))
                            act.wait_ge(ab_made, this(n, 1))
                            act.copy(ab[:], pAB[:, 0:T * 16].rearrange("p (t e) -> p t e", t=T)).then_inc(ab_ready, 1)
                        if m - 2 in gate_after:
                            t = gate_after[m - 2]
                            act.wait_ge(g_made, this(n, T, t + 1))
                            act.wait_ge(g_ready, this(n, T, t - 1))
                            act.activation(gate[:, t % 2], pG[:, t % 2], AF.Silu).then_inc(g_silu, 1)
                    for v in range(MV):
                        copy_v(act, n, v)
                    act.wait_ge(nsq_stored, last(n, 16))
                    act.wait_ge(summed, this(n, MQK))
                    act.copy(nsq[:], pN[:, 0:T * MQK].rearrange("p (t m) -> p t m", t=T)).then_inc(nsq_ready, 1)

        @block.vector
        def _(dve):
            for q, per in ((conv_done, M), (g_ready, T)):
                dve.sem_inc(q, per)
            dve.memset(ones[:], 1.0).then_inc(ones_set, 1)
            dve.wait_ge(weights_in, 16 * len(consts))
            with dve.Fori(0, B) as b:
                for s in range(2):
                    n = b * 2 + s
                    for first in range(0, M, 2):
                        for m in (first, first + 1):
                            dve.wait_ge(p_copied, this(n, M, m + 1))
                            if s == 0:
                                dve.memset(raw[:, m % 4, 0:3], 0.0).then_inc(tile_step[m % 2], 1)
                            else:
                                dve.tensor_copy(raw[:, m % 4, 0:3], tail[:, m, 0:3]).then_inc(tile_step[m % 2], 1)
                        for tap in (2, 1, 0):
                            for m in (first, first + 1):
                                dve.wait_ge(tile_step[m % 2], 1)
                                dve.sem_inc(tile_step[m % 2], -1)
                                dve.scalar_tensor_tensor(y[:, m % 4], raw[:, m % 4, tap:C + tap], taps[:, m, tap:tap + 1], y[:, m % 4],
                                                         ALU.mult, ALU.add).then_inc(tile_step[m % 2], 1)
                        for m in (first, first + 1):
                            dve.tensor_copy(tail[:, m, 0:3], raw[:, m % 4, C:C + 3])
                            dve.wait_ge(tile_step[m % 2], 1)
                            dve.sem_inc(tile_step[m % 2], -1)
                            dve.tensor_scalar_max(y[:, m % 4], y[:, m % 4], LEAST_LOGIT).then_inc(conv_done, 1)
                        if first - 2 in gate_after:
                            t = gate_after[first - 2]
                            if t == 0:
                                dve.wait_ge(g_stored, last(n, 16))
                            dve.wait_ge(g_silu, this(n, T, t + 1))
                            dve.tensor_tensor(gate_w[:, t], gate[:, t % 2], norm_w[:], ALU.mult).then_inc(g_ready, 1)


def make_decays(nc, w, ab_d, alpha_d, beta_d):
    NT, H = alpha_d.shape[0], 8
    with ExitStack() as ctx:
        sb, ps, sem = _memory(nc, ctx, "h_")
        ident = sb("ident", [P, P])
        ab = sb("ab", [P, NT, 2 * H])
        dt_bias = sb("dt_bias", [P, H])
        a_log = sb("a_log", [P, H])
        z, zn, u, s_, s2, acc = (sb(x, [P, NT, H]) for x in ("z", "zn", "u", "s", "s2", "acc"))
        alpha = sb("alpha", [P, NT * H])
        beta = sb("beta", [P, NT * H])
        aT = sb("aT", [P, NT * H // P, P])
        pA = ps("pA", [P, NT * H // P, P])
        loaded, dstep, astep, z_ready, u_ready, g_ready, alpha_ready, beta_ready = (
            sem(x) for x in ("loaded", "dstep", "astep", "z_ready", "u_ready", "g_ready", "alpha_ready", "beta_ready"))
        turned, aT_ready, stored, beta_raw = sem("turned"), sem("aT_ready"), sem("stored"), sem("beta_raw")
        block = ctx.enter_context(nc.Block())

        @block.sync
        def _(sp):
            sp.dma_start(ident[:], w["ident"]).then_inc(loaded, 16)
            sp.dma_start(ab[:], ab_d.rearrange("(t p) e -> p t e", p=P)).then_inc(loaded, 16)
            sp.dma_start(dt_bias[:], w["dt_bias"]).then_inc(loaded, 16)
            sp.dma_start(a_log[:], w["a_log"]).then_inc(loaded, 16)
            sp.wait_ge(beta_ready, 1)
            sp.dma_start(beta_d.rearrange("(t p) h -> p t h", p=P), beta[:].rearrange("p (t h) -> p t h", h=H)).then_inc(stored, 16)
            sp.wait_ge(aT_ready, 1)
            sp.dma_start(alpha_d.rearrange("(g q) h n -> (q h) g n", q=P // H), aT[:]).then_inc(stored, 16)
            sp.wait_ge(stored, 32)

        @block.vector
        def _(dve):
            wide = [P, NT, H]
            dve.wait_ge(loaded, 64)
            after(dve, dstep, dve.tensor_tensor(z[:], ab[:, :, 0:H], dt_bias[:].unsqueeze(1).to_broadcast(wide), ALU.add))
            after(dve, dstep, dve.tensor_scalar(zn[:], z[:], -1.0, None, ALU.mult))
            dve.tensor_tensor(zn[:], zn[:], z[:], ALU.min).then_inc(z_ready, 1)
            dve.wait_ge(u_ready, 1)
            after(dve, dstep, dve.tensor_scalar_add(s_[:], u[:], 2.0))
            after(dve, dstep, dve.reciprocal(s_[:], s_[:]))
            after(dve, dstep, dve.tensor_tensor(s_[:], s_[:], u[:], ALU.mult))
            after(dve, dstep, dve.tensor_tensor(s2[:], s_[:], s_[:], ALU.mult))
            after(dve, dstep, dve.tensor_scalar(acc[:], s2[:], 2.0 / 19, 2.0 / 17, ALU.mult, ALU.add))
            for k in range(15, 0, -2):
                after(dve, dstep, dve.tensor_tensor(acc[:], acc[:], s2[:], ALU.mult))
                after(dve, dstep, dve.tensor_scalar_add(acc[:], acc[:], 2.0 / k))
            after(dve, dstep, dve.tensor_tensor(acc[:], acc[:], s_[:], ALU.mult))
            after(dve, dstep, dve.tensor_scalar_max(z[:], z[:], 0.0))
            after(dve, dstep, dve.tensor_tensor(acc[:], acc[:], z[:], ALU.add))
            after(dve, dstep, dve.tensor_tensor(acc[:], acc[:], a_log[:].unsqueeze(1).to_broadcast(wide), ALU.mult))
            dve.tensor_scalar(acc[:], acc[:], -1.0, None, ALU.mult).then_inc(g_ready, 1)
            dve.wait_ge(beta_raw, 1)
            dve.tensor_scalar(beta[:], beta[:], 2.0, None, ALU.mult).then_inc(beta_ready, 1)

        @block.scalar
        def _(act):
            act.wait_ge(loaded, 64)
            act.activation(a_log[:], a_log[:], AF.Exp)
            act.wait_ge(z_ready, 1)
            act.activation(u[:], zn[:], AF.Exp).then_inc(u_ready, 1)
            act.wait_ge(g_ready, 1)
            act.activation(alpha[:].rearrange("p (t h) -> p t h", h=H), acc[:], AF.Exp).then_inc(alpha_ready, 1)
            act.activation(beta[:].rearrange("p (t h) -> p t h", h=H), ab[:, :, H:], AF.Sigmoid).then_inc(beta_raw, 1)
            act.wait_ge(turned, 1)
            act.copy(aT[:], pA[:]).then_inc(aT_ready, 1)

        @block.tensor
        def _(pe):
            pe.wait_ge(alpha_ready, 1)
            for g in range(NT * H // P):
                mm = pe.transpose(pA[:, g], alpha[:, g * P:(g + 1) * P], ident[:])
            mm.then_inc(turned, 1)

TINY = 1e-19


def delta_rule(nc, w, kq_d, v_d, silu_gate_d, nsq_d, alpha_d, beta_d, o_d):
    NT = kq_d.shape[0]
    H, V = 8, 64
    B, HG = 8, 4
    L = 7
    with ExitStack() as ctx:
        sb, ps, sem = _memory(nc, ctx, "j_")
        ident = sb("ident", [P, P])
        eye = sb("eye", [P, H, P])
        joins = sb("joins", [P, 2, L, HG * P], I32)
        minus_half = sb("minus_half", [P, 2 * H])
        kq = sb("kq", [P, 2, H, 2, P])
        v = sb("v", [P, 2, H, V])
        gate = sb("gate", [P, 2, H, V])
        nsq = sb("nsq", [P, 2, H, 2])
        beta = sb("beta", [P, 2, H])
        al = sb("al", [P, 2, H, P])
        a0 = sb("a0", [P, H])
        dT = sb("dT", [P, 2, H, P])
        ones = sb("ones", [P, P])
        g_end = sb("g_end", [P, H])
        rn = sb("rn", [P, 2, H, 2])
        nsqm = sb("nsqm", [P, H, 2])
        br = sb("br", [P, H])
        nbr2 = sb("nbr2", [P, H])
        cg = sb("cg", [P, H])
        gam = sb("gam", [P, 2, H])
        at = sb("at", [P, H, P])
        pt = sb("pt", [P, H, P])
        na = sb("na", [P, H, P])
        kn = sb("kn", [P, H, P])
        X = sb("X", [P, H, P])
        T = sb("T", [P, H, P])
        q1 = sb("q1", [P, H, P])
        S = sb("S", [P, H, V])
        wv = sb("wv", [P, H, V])
        u = sb("u", [P, H, V])
        ud = sb("ud", [P, H, V])
        o = sb("o", [P, H, V])
        oo = sb("oo", [P, H, V])
        ss = sb("ss", [P, H])
        rr = sb("rr", [P, H])
        on = sb("on", [P, H, V])
        pB = ps("pB", [P, 4, 512])
        pC = ps("pC", [P, 2, 512])
        pS = ps("pS", [P, 2, 512])
        names = ("consts_in ones_set nsq_ok rn_ready dt_ready nb_ready kq_made at_ready kn_turned kn_ready a_turned na_ready nt_turned "
                 "x_ready t_ready q1_made q1_ready x_made t_made gam_made gam_ready ks_made qs_made s_reset s_ready w_ready o_begun "
                 "u_made u_ready ud_ready o_made s_made o_ready ss_ready rr_ready on_ready on_stored eye_set turns_begun joins_begun g_end_ready dve_step pool_step").split()
        q_ = {name: sem(name) for name in names}
        ins = [sem("in0"), sem("in1")]
        (consts_in, ones_set, nsq_ok, rn_ready, dt_ready, nb_ready, kq_made, at_ready, kn_turned, kn_ready, a_turned, na_ready,
         nt_turned, x_ready, t_ready, q1_made, q1_ready, x_made, t_made, gam_made, gam_ready, ks_made, qs_made, s_reset, s_ready,
         w_ready, o_begun, u_made, u_ready, ud_ready, o_made, s_made, o_ready, ss_ready, rr_ready, on_ready, on_stored,
         eye_set, turns_begun, joins_begun, g_end_ready, dve_step, pool_step) = (q_[name] for name in names)
        block = ctx.enter_context(nc.Block())
        ntd = nsq_d.rearrange("(n p) e -> n p e", p=P)
        bt = beta_d.rearrange("(n p) e -> n p e", p=P)
        vt = v_d.rearrange("(n p) e -> n p e", p=P)
        gt = silu_gate_d.rearrange("(n p) e -> n p e", p=P)
        ot = o_d.rearrange("(n p) e -> n p e", p=P)

        def flat(t):
            return t.rearrange("p h n -> p (h n)")

        @block.sync
        def _(sp):
            sp.sem_inc(on_stored, 16)
            for dst, name in ((ident, "ident"), (eye, "eye"), (joins, "joins")):
                sp.dma_start(dst[:], w[name]).then_inc(consts_in, 16)

            def load(n, s):
                for dst, src in ((kq[:, s], kq_d[n]), (flat(al[:, s]), alpha_d[n].rearrange("h n -> (h n)").unsqueeze(0).to_broadcast([P, H * P])),
                                 (nsq[:, s].rearrange("p h s -> p (h s)"), ntd[n]), (beta[:, s], bt[n]),
                                 (flat(v[:, s]), vt[n]), (flat(gate[:, s]), gt[n])):
                    sp.dma_start(dst, src).then_inc(ins[s], 16)

            def pair(m, ends):
                for s in range(2):
                    n = m * 2 + s
                    if not (ends and s):
                        sp.wait_ge(on_ready, last(n, 1))
                        load(n + 1, 1 - s)
                    sp.wait_ge(on_ready, this(n, 1))
                    sp.dma_start(ot[n], flat(on[:])).then_inc(on_stored, 16)

            load(0, 0)
            with sp.Fori(0, NT // 2 - 1) as m:
                pair(m, False)
            pair(NT // 2 - 1, True)
            sp.wait_ge(on_stored, this(NT - 1, 16))

        @block.gpsimd
        def _(pool):
            for q in (rn_ready, eye_set, rr_ready):
                pool.sem_inc(q, 1)
            after(pool, pool_step, pool.memset(minus_half[:], -0.5))
            pool.wait_ge(consts_in, 48)

            def begin_inverses():
                pool.sem_inc(turns_begun, 1)
                pool.tensor_copy(X[:], eye[:])
                pool.tensor_copy(T[:], eye[:]).then_inc(eye_set, 1)

            def norms(n, s):
                pool.wait_ge(nsq_ok, this(n, 1))
                pool.tensor_tensor(flat(rn[:, s]), flat(nsqm[:]), minus_half[:], ALU.pow).then_inc(rn_ready, 1)

            def turn(n, s, more):
                if more:
                    pool.wait_ge(on_ready, last(n, 1))
                    norms(n + 1, 1 - s)
                pool.wait_ge(u_made, this(n, 1))
                pool.wait_ge(t_ready, this(n, 2 * (L - 1)))
                if more:
                    begin_inverses()
                pool.wait_ge(ss_ready, this(n, 1))
                pool.tensor_tensor(rr[:], ss[:], minus_half[:, 0:H], ALU.pow).then_inc(rr_ready, 1)

            begin_inverses()
            norms(0, 0)
            with pool.Fori(0, NT // 2 - 1) as m:
                for s in range(2):
                    turn(m * 2 + s, s, True)
            for s in range(2):
                turn(NT - 2 + s, s, s == 0)

        @block.tensor
        def _(pe):
            for q, per in ((kq_made, 4), (kn_turned, 2), (a_turned, 2), (nt_turned, 2), (q1_made, 2 * (L - 1)), (x_made, 2 * (L - 1)),
                           (t_made, 2 * (L - 2)), (gam_made, 1), (ks_made, 1), (qs_made, 1), (u_made, 1), (o_made, 1), (s_made, 1)):
                pe.sem_inc(q, per)
            pe.wait_ge(consts_in, 48)
            pe.wait_ge(ones_set, 1)

            def turn(b, n, s):
                pe.wait_ge(ins[s], (n - s) * 48 + 96)
                for q in range(4):
                    pe.wait_ge(x_ready, last(n, 2 * L))
                    for h in (2 * q, 2 * q + 1):
                        mm = pe.matmul(pB[:, q, (h % 2) * 256:(h % 2 + 1) * 256], kq[:, s, h, 0, :],
                                       kq[:, s, h].rearrange("p s n -> p (s n)"), start=True, stop=True)
                    mm.then_inc(kq_made, 1)
                pe.wait_ge(t_ready, last(n, 2 * (L - 1)))
                for g in range(2):
                    for h in range(HG):
                        mm = pe.transpose(pC[:, g, h * P:(h + 1) * P], kq[:, s, g * HG + h, 0, :], ident[:])
                    mm.then_inc(kn_turned, 1)
                pe.wait_ge(dt_ready, this(n, 1))
                pe.wait_ge(s_ready, last(n, 1))
                for h in range(H):
                    pe.matmul(pS[:, 0, h:h + 1], dT[0:1, s, h, :], a0[0:1, h:h + 1], start=True, stop=True)
                pe.wait_ge(g_end_ready, this(n, 1))
                pe.matmul(pS[:, 0, H:2 * H], ones[0:1], g_end[0:1], start=True, stop=True).then_inc(gam_made, 1)
                for g in range(2):
                    pe.wait_ge(at_ready, this(n, 4, 2 * g + 2))
                    for h in range(HG):
                        mm = pe.transpose(pB[:, 2 * g, h * P:(h + 1) * P], at[:, g * HG + h, :], ident[:])
                    mm.then_inc(a_turned, 1)
                for g in range(2):
                    pe.wait_ge(na_ready, this(n, 2, g + 1))
                    for h in range(HG):
                        mm = pe.transpose(pB[:, 2 * g + 1, h * P:(h + 1) * P], na[:, g * HG + h, :], ident[:])
                    mm.then_inc(nt_turned, 1)
                pe.wait_ge(s_reset, b + 1)
                pe.wait_ge(gam_ready, this(n, 1))
                for h in range(H):
                    mm = pe.matmul(pS[:, 0, h * V:(h + 1) * V], kq[:, s, h, 0, :], S[:, h, :], start=True, stop=True)
                mm.then_inc(ks_made, 1)
                pe.wait_ge(o_ready, last(n, 1))
                for h in range(H):
                    mm = pe.matmul(pS[:, 1, h * V:(h + 1) * V], kq[:, s, h, 1, :], S[:, h, :], start=True, stop=True)
                mm.then_inc(qs_made, 1)
                pe.wait_ge(kn_ready, this(n, 2))
                for l in range(1, L):
                    for g in range(2):
                        pe.wait_ge(x_ready, this(n, 2 * L, 2 * l if l == 1 else 2 * (l - 1) + g + 1))
                        for h in range(g * HG, g * HG + HG):
                            mm = pe.matmul(pB[:, g, (h % HG) * P:(h % HG + 1) * P], na[:, h, :], X[:, h, :], start=True, stop=True)
                        mm.then_inc(q1_made, 1)
                    for g in range(2):
                        pe.wait_ge(q1_ready, this(n, 2 * (L - 1), 2 * (l - 1) + g + 1))
                        pe.wait_ge(t_ready, this(n, 2 * (L - 1), 2 * (l - 1) + g + 1))
                        for h in range(g * HG, g * HG + HG):
                            mm = pe.matmul(pB[:, 2 + g, (h % HG) * P:(h % HG + 1) * P], T[:, h, :], q1[:, h, :], start=True, stop=True)
                        mm.then_inc(x_made, 1)
                        if l < L - 1:
                            for h in range(g * HG, g * HG + HG):
                                mm = pe.matmul(pC[:, g, (h % HG) * P:(h % HG + 1) * P], q1[:, h, :], T[:, h, :], start=True, stop=True)
                            mm.then_inc(t_made, 1)
                pe.wait_ge(w_ready, this(n, 1))
                pe.wait_ge(x_ready, this(n, 2 * L))
                for h in range(H):
                    mm = pe.matmul(pS[:, 0, h * V:(h + 1) * V], X[:, h, :], wv[:, h, :], start=True, stop=True)
                mm.then_inc(u_made, 1)
                pe.wait_ge(u_ready, this(n, 1))
                pe.wait_ge(o_begun, this(n, 1))
                for h in range(H):
                    mm = pe.matmul(pS[:, 1, h * V:(h + 1) * V], pt[:, h, :], u[:, h, :], start=True, stop=True)
                mm.then_inc(o_made, 1)
                pe.wait_ge(ud_ready, this(n, 1))
                for h in range(H):
                    mm = pe.matmul(pS[:, 0, h * V:(h + 1) * V], kn[:, h, :], ud[:, h, :], start=True, stop=True)
                mm.then_inc(s_made, 1)

            with pe.Fori(0, B) as b:
                with pe.Fori(0, NT // B // 2) as c:
                    for s in range(2):
                        turn(b, b * (NT // B) + c * 2 + s, s)

        @block.scalar
        def _(act):
            for q, per in ((kn_ready, 2), (gam_ready, 1), (na_ready, 2), (q1_ready, 2 * (L - 1)), (u_ready, 1)):
                act.sem_inc(q, per)
            with act.Fori(0, NT) as n:
                act.wait_ge(s_made, last(n, 1))
                for g in range(2):
                    act.wait_ge(kn_turned, this(n, 2, g + 1))
                    act.copy(flat(kn[:, g * HG:(g + 1) * HG]), pC[:, g]).then_inc(kn_ready, 1)
                act.wait_ge(gam_made, this(n, 1))
                act.copy(gam[:].rearrange("p s h -> p (s h)"), pS[:, 0, 0:2 * H]).then_inc(gam_ready, 1)
                act.wait_ge(nb_ready, this(n, 1))
                for g in range(2):
                    act.wait_ge(a_turned, this(n, 2, g + 1))
                    for h in range(g * HG, g * HG + HG):
                        cp = act.activation(na[:, h], pB[:, 2 * g, (h % HG) * P:(h % HG + 1) * P], AF.Copy, scale=nbr2[:, h:h + 1])
                    cp.then_inc(na_ready, 1)
                for l in range(1, L):
                    for g in range(2):
                        act.wait_ge(q1_made, this(n, 2 * (L - 1), 2 * (l - 1) + g + 1))
                        if l > 1:
                            act.wait_ge(*((t_made, this(n, 2 * (L - 2), 2 * (l - 2) + g + 1))))
                        act.copy(flat(q1[:, g * HG:(g + 1) * HG]), pB[:, g]).then_inc(q1_ready, 1)
                act.wait_ge(u_made, this(n, 1))
                act.copy(flat(u[:]), pS[:, 0]).then_inc(u_ready, 1)

        def heads(col):
            return col.unsqueeze(2).to_broadcast([P, H, V])

        @block.vector
        def _(dve):
            for q, per in ((nsq_ok, 1), (dt_ready, 1), (nb_ready, 1), (at_ready, 4), (x_ready, 2 * L), (t_ready, 2 * (L - 1)), (s_ready, 1),
                           (w_ready, 1), (o_begun, 1), (ud_ready, 1), (o_ready, 1), (ss_ready, 1), (on_ready, 1),
                           (g_end_ready, 1)):
                dve.sem_inc(q, per)
            dve.memset(ones[:], 1.0).then_inc(ones_set, 1)
            dve.wait_ge(consts_in, 48)
            pS0 = pS[:, 0].rearrange("p (h v) -> p h v", h=H)
            pS1 = pS[:, 1].rearrange("p (h v) -> p h v", h=H)

            def decays(n, s):
                dve.wait_ge(ins[s], (n - s) * 48 + 96)
                dve.wait_ge(rn_ready, last(n, 1))
                dve.tensor_scalar_max(nsqm[:], nsq[:, s], 1e-12).then_inc(nsq_ok, 1)
                dve.wait_ge(gam_made, last(n, 1))
                after(dve, dve_step, dve.tensor_copy(a0[:], al[:, s, :, 0]))
                after(dve, dve_step, dve.memset(al[:, s, :, 0:1], 0.0))
                after(dve, dve_step, dve.tensor_tensor_scan(flat(dT[:, s]), flat(al[:, s]), flat(eye[:]), 0.0, ALU.mult, ALU.add))
                dve.scalar_tensor_tensor(dT[:, s], dT[:, s], TINY, dT[:, s], ALU.is_ge, ALU.mult).then_inc(dt_ready, 1)
                dve.wait_ge(dt_ready, this(n, 1))
                dve.tensor_tensor(g_end[0:1], dT[0:1, s, :, P - 1], a0[0:1], ALU.mult).then_inc(g_end_ready, 1)

            def turn(n, s, more):
                dve.wait_ge(rn_ready, this(n, 1))
                after(dve, dve_step, dve.tensor_tensor(br[:], beta[:, s], rn[:, s, :, 0], ALU.mult))
                dve.scalar_tensor_tensor(nbr2[:], br[:], -1.0, rn[:, s, :, 0], ALU.mult, ALU.mult).then_inc(nb_ready, 1)
                dve.wait_ge(dt_ready, this(n, 1))
                dve.wait_ge(o_made, last(n, 1))
                for q in range(4):
                    dve.wait_ge(kq_made, this(n, 4, q + 1))
                    hs = slice(2 * q, 2 * q + 2)
                    both = pB[:, q].rearrange("p (h s n) -> p h s n", h=2, s=2)
                    dve.tensor_tensor(at[:, hs], both[:, :, 0], dT[:, s, hs], ALU.mult)
                    dve.tensor_tensor(pt[:, hs], both[:, :, 1], dT[:, s, hs], ALU.mult).then_inc(at_ready, 1)
                dve.wait_ge(eye_set, this(n, 1))
                for g in range(2):
                    gs = slice(g * HG, g * HG + HG)
                    dve.wait_ge(na_ready, this(n, 2, g + 1))
                    dve.sem_inc(joins_begun, 1)
                    dve.copy_predicated(flat(T[:, gs]), joins[:, 0, 0], flat(na[:, gs])).then_inc(t_ready, 1)
                    dve.wait_ge(nt_turned, this(n, 2, g + 1))
                    dve.sem_inc(joins_begun, 1)
                    dve.copy_predicated(flat(X[:, gs]), joins[:, 1, 0], pB[:, 2 * g + 1]).then_inc(x_ready, 1)
                dve.wait_ge(gam_ready, this(n, 1))
                dve.wait_ge(nb_ready, this(n, 1))
                dve.tensor_tensor(cg[:], nbr2[:], gam[:, 0], ALU.mult)
                after(dve, dve_step, dve.tensor_tensor(wv[:], v[:, s], heads(br[:]), ALU.mult))
                dve.wait_ge(ks_made, this(n, 1))
                after(dve, dve_step, dve.tensor_tensor(ud[:], pS0, heads(cg[:]), ALU.mult))
                dve.tensor_tensor(wv[:], wv[:], ud[:], ALU.add).then_inc(w_ready, 1)
                dve.wait_ge(qs_made, this(n, 1))
                dve.tensor_tensor(o[:], pS1, heads(gam[:, 0]), ALU.mult).then_inc(o_begun, 1)
                for l in range(1, L):
                    for g in range(2):
                        gs = slice(g * HG, g * HG + HG)
                        dve.wait_ge(x_made, this(n, 2 * (L - 1), 2 * (l - 1) + g + 1))
                        dve.sem_inc(joins_begun, 1)
                        dve.copy_predicated(flat(X[:, gs]), joins[:, 1, l], pB[:, 2 + g]).then_inc(x_ready, 1)
                        if l < L - 1:
                            dve.wait_ge(t_made, this(n, 2 * (L - 2), 2 * (l - 1) + g + 1))
                            dve.sem_inc(joins_begun, 1)
                            dve.copy_predicated(flat(T[:, gs]), joins[:, 0, l], pC[:, g]).then_inc(t_ready, 1)
                    if l == 4 and more:
                        decays(n + 1, 1 - s)
                dve.wait_ge(u_ready, this(n, 1))
                dve.tensor_tensor(ud[:], u[:], dT[:, s, :, P - 1:P].to_broadcast([P, H, V]), ALU.mult).then_inc(ud_ready, 1)
                after(dve, dve_step, dve.tensor_tensor(S[:], S[:], heads(gam[:, 1]), ALU.mult))
                dve.wait_ge(s_made, this(n, 1))
                dve.tensor_tensor(S[:], pS0, S[:], ALU.add).then_inc(s_ready, 1)
                dve.wait_ge(o_made, this(n, 1))
                after(dve, dve_step, dve.tensor_tensor(o[:], pS1, o[:], ALU.add))
                dve.tensor_tensor(o[:], o[:], heads(rn[:, s, :, 1]), ALU.mult).then_inc(o_ready, 1)
                dve.wait_ge(o_ready, this(n, 1))
                after(dve, dve_step, dve.tensor_tensor(oo[:], o[:], o[:], ALU.mult))
                after(dve, dve_step, dve.tensor_reduce(ss[:], oo[:], AX.X, ALU.add))
                dve.tensor_scalar(ss[:], ss[:], 1.0 / V, 1e-5, ALU.mult, ALU.add).then_inc(ss_ready, 1)
                dve.wait_ge(rr_ready, this(n, 1))
                dve.wait_ge(on_stored, last(n, 16))
                after(dve, dve_step, dve.tensor_tensor(on[:], o[:], heads(rr[:]), ALU.mult))
                dve.tensor_tensor(on[:], on[:], gate[:, s], ALU.mult).then_inc(on_ready, 1)

            def empty_state(b):
                dve.wait_ge(s_ready, b * (NT // B) + 1)
                dve.memset(S[:], 0.0).then_inc(s_reset, 1)

            decays(0, 0)
            with dve.Fori(0, B - 1) as b:
                empty_state(b)
                with dve.Fori(0, NT // B // 2) as c:
                    for s in range(2):
                        turn(b * (NT // B) + c * 2 + s, s, True)
            empty_state(B - 1)
            with dve.Fori(0, NT // B // 2 - 1) as c:
                for s in range(2):
                    turn(NT - NT // B + c * 2 + s, s, True)
            for s in range(2):
                turn(NT - 2 + s, s, s == 0)


def finish_l1(nc, w, o_d, x1_d, gate_d, out):
    B, N, D = out.shape
    C, V = 512, 512
    T, K4 = C // P, V // P
    with ExitStack() as ctx:
        sb, ps, sem = _memory(nc, ctx, "i_")
        ident = sb("ident", [P, P])
        wo = sb("wo", [P, K4, D])
        o = sb("o", [P, 2, T, V])
        x1 = sb("x1", [P, 2, T, D])
        gate = sb("gate", [P, 2, T, D])
        oT = sb("oT", [P, K4, C])
        y = sb("y", [P, T, D])
        pT = ps("pT", [P, K4, C])
        pY = ps("pY", [P, 2, 512])
        weights_in, in_, stored = sem("weights_in"), [sem("in0"), sem("in1")], sem("stored")
        turned, oT_ready, made, gated, y_ready = sem("turned"), sem("oT_ready"), sem("made"), sem("gated"), sem("y_ready")
        y_free = sem("y_free")
        block = ctx.enter_context(nc.Block())

        def tiles(a):
            return a.rearrange("(b c t p) d -> b c p t d", b=B, c=2, p=P)

        ot, xt, gt = tiles(o_d), tiles(x1_d), tiles(gate_d)
        yt = out.rearrange("b (c t p) d -> b c p t d", c=2, p=P)

        @block.sync
        def _(sp):
            sp.dma_start(ident[:], w["ident"]).then_inc(weights_in, 16)
            sp.dma_start(wo[:], w["wo1"]).then_inc(weights_in, 16)
            with sp.Fori(0, B) as b:
                for s in range(2):
                    n = b * 2 + s
                    sp.wait_ge(y_ready, last(n, 1, 0) + 1)
                    sp.dma_start(o[:, s], ot[b, s]).then_inc(in_[s], 16)
                    sp.dma_start(x1[:, s], xt[b, s]).then_inc(in_[s], 16)
                    sp.dma_start(gate[:, s], gt[b, s]).then_inc(in_[s], 16)

        @block.gpsimd
        def _(pool):
            pool.sem_inc(y_free, 1)
            with pool.Fori(0, B) as b:
                for s in range(2):
                    n = b * 2 + s
                    pool.wait_ge(y_ready, this(n, 1) + 1)
                    pool.dma_start(yt[b, s], y[:]).then_inc(stored, 16)
                    pool.wait_ge(stored, n * 16 + 16)
                    pool.sem_inc(y_free, 1)
            pool.wait_ge(stored, 32 * B)

        @block.tensor
        def _(pe):
            for q, per in ((turned, 1), (made, T)):
                pe.sem_inc(q, per)
            pe.wait_ge(weights_in, 32)
            with pe.Fori(0, B) as b:
                for s in range(2):
                    n = b * 2 + s
                    pe.wait_ge(in_[s], b * 48 + 48)
                    pe.wait_ge(oT_ready, last(n, 1))
                    for k in range(K4):
                        for t in range(T):
                            mm = pe.transpose(pT[:, k, t * P:(t + 1) * P], o[:, s, t, k * P:(k + 1) * P], ident[:])
                    mm.then_inc(turned, 1)
                    pe.wait_ge(oT_ready, this(n, 1))
                    for t in range(T):
                        pe.wait_ge(gated, this(n, T, t - 1))
                        for k in range(K4):
                            mm = pe.matmul(pY[:, t % 2, 0:D], oT[:, k, t * P:(t + 1) * P], wo[:, k, :], start=k == 0, stop=k == K4 - 1)
                        mm.then_inc(made, 1)

        @block.scalar
        def _(act):
            act.sem_inc(oT_ready, 1)
            with act.Fori(0, B) as b:
                for s in range(2):
                    n = b * 2 + s
                    act.wait_ge(turned, this(n, 1))
                    act.wait_ge(made, last(n, T))
                    for k in range(K4):
                        cp = act.copy(oT[:, k], pT[:, k])
                    cp.then_inc(oT_ready, 1)

        @block.vector
        def _(dve):
            dve.sem_inc(y_ready, 2)
            dve.sem_inc(gated, T)
            with dve.Fori(0, B) as b:
                for s in range(2):
                    n = b * 2 + s
                    dve.wait_ge(y_free, last(n, 1))
                    for t in range(T):
                        dve.wait_ge(made, this(n, T, t + 1))
                        dve.tensor_tensor(y[:, t], pY[:, t % 2, 0:D], gate[:, s, t], ALU.mult).then_inc(gated, 1)
                    dve.wait_ge(gated, this(n, T))
                    dve.tensor_tensor(y[:], y[:], x1[:, s], ALU.add).then_inc(y_ready, 1)


def two_layers(nc, x, w, out):
    def dram(name, shape, dt=F32):
        return nc.dram_tensor(name, shape, dt, kind="Internal").ap()

    xn_d, ffn_d = dram("normed", [8192, 256]), dram("ffn_sum", [8192, 256])
    qk_d, v0_d = dram("queries_keys", [8, 2, 3, 256, 1024], BF16), dram("values", [8, 1024, 272])
    score_d = dram("router_scores", [8, 16, 1024])
    idx_d, wt_d = dram("chosen_tokens", [128, 128], U32), dram("chosen_weights", [128, 128])
    att_d = dram("attended", [8192, 256])
    x1_d, xnT_d, gate_d = dram("layer0_out", [8192, 256]), dram("normed1_turned", [256, 8192]), dram("gate1", [8192, 256])
    kq_d, v1_d = dram("delta_keys_queries", [64, 128, 8, 2, 128]), dram("delta_values", [8192, 512])
    silu_gate_d, nsq_d, ab_d = dram("silu_gate", [8192, 512]), dram("squared_norms", [8192, 16]), dram("alpha_beta_logits", [8192, 16])
    alpha_d, beta_d = dram("alpha", [64, 8, 128]), dram("beta", [8192, 8])
    o_d = dram("delta_out", [8192, 512])

    project_l0(nc, x, w, xn_d, qk_d, v0_d, score_d, ffn_d)
    choose_tokens(nc, w, score_d, idx_d, wt_d)
    attend(nc, w, qk_d, v0_d, att_d)
    run_experts(nc, w, xn_d, idx_d, wt_d, ffn_d)
    finish_l0(nc, x, w, att_d, ffn_d, x1_d, xnT_d, gate_d)
    project_l1(nc, w, xnT_d, kq_d, v1_d, silu_gate_d, nsq_d, ab_d)
    make_decays(nc, w, ab_d, alpha_d, beta_d)
    delta_rule(nc, w, kq_d, v1_d, silu_gate_d, nsq_d, alpha_d, beta_d, o_d)
    finish_l1(nc, w, o_d, x1_d, gate_d, out)


def layout(a):
    D = 256

    def rows(m):
        return m.reshape(-1, P, m.shape[1]).transpose(1, 0, 2)

    def spread(v):
        return np.broadcast_to(v, (P,) + v.shape)

    qkv = a["L0_attn_attn_W"].reshape(D, 16, 3, 16)
    qkvb = a["L0_attn_attn_b"].reshape(16, 3, 16)
    w = {}
    w["ident"] = np.eye(P, dtype=np.float32)
    w["first_row"] = (np.arange(P, dtype=np.float32).reshape(P, 1) // 16) * 1024
    key_after = np.triu(np.ones((P, P), np.float32), 1)
    w["mask1"] = (key_after * -30000).astype(np.float32)
    w["mask2"] = (key_after.T * -30000).astype(np.float32)
    w["blocks"] = np.repeat(np.tile(np.eye(8), (16, 1))[:, :, None], P, 2).astype(np.float32)
    w["gather"] = np.tile(np.eye(32, 17, dtype=np.float32), (4, 1))
    w["wqk"] = rows(qkv[:, :, 0:2].transpose(0, 2, 1, 3).reshape(D, 2 * D)).reshape(P, 2, 4, P)
    w["bqk"] = qkvb[:, 0:2].transpose(1, 0, 2).reshape(4, P).T
    w["wv"] = rows(qkv[:, :, 2].reshape(D, D))
    w["bv"] = spread(qkvb[:, 2].reshape(D))
    w["wr"] = rows(a["L0_ffn_gate_w"].T)
    w["wg"] = rows(a["L0_ffn_Ws_g"].T).reshape(P, 2, 4, P)
    w["wu"] = rows(a["L0_ffn_Ws_u"].T).reshape(P, 2, 4, P)
    w["wd"] = rows(a["L0_ffn_Ws_d"].T)
    for name, m in (("Wg", a["L0_ffn_Wg"]), ("Wu", a["L0_ffn_Wu"])):
        w[name] = m.transpose(0, 2, 1).reshape(16, 2, P, 512).transpose(0, 2, 1, 3).reshape(16, P, 2, 4, P)
    w["Wd"] = a["L0_ffn_Wd"].transpose(0, 2, 1).reshape(16, 4, P, D).transpose(0, 2, 1, 3)
    for name, s, r in (("wg1", "L1_ffn_wg_s", "L1_ffn_wg_r"), ("wu1", "L1_ffn_wu_s", "L1_ffn_wu_r")):
        m = np.concatenate([a[s].transpose(1, 0, 2).reshape(D, 256), a[r].transpose(1, 0, 2).reshape(D, 1024)], 1)
        w[name] = rows(m).reshape(P, 2, 10, P)
    w["wd1"] = rows(np.concatenate([a["L1_ffn_wd_s"].reshape(256, D), a["L1_ffn_wd_r"].reshape(1024, D)], 0))
    w["wo"] = rows(a["L0_attn_out_W"])
    w["bo"] = spread(a["L0_attn_out_b"])
    w["wr1"] = rows(a["L1_ffn_router_w"])
    w["spread"] = (np.arange(16)[:, None] == (np.arange(1024) // 64)).astype(np.float32).reshape(16, 8, P)
    w["iota"] = spread(np.arange(16, dtype=np.float32))
    def by_head(k, q, v):
        kq = np.stack([k.reshape(-1, 8, P), q.reshape(-1, 8, P)], 2)
        return np.concatenate([kq.reshape(k.shape[0], 16 * P), v], 1)

    w["wp"] = rows(by_head(a["L1_attn_Wk"], a["L1_attn_Wq"], a["L1_attn_Wv"])).reshape(P, 2, 20, P)
    taps = by_head(a["L1_attn_conv_k"].T, a["L1_attn_conv_q"].T, a["L1_attn_conv_v"].T)
    w["taps"] = taps.reshape(4, 20, P).transpose(2, 1, 0)
    w["wgate"] = rows(a["L1_attn_Wg"])
    w["wab"] = rows(np.concatenate([a["L1_attn_Wa"], a["L1_attn_Wb"]], 1))
    w["norm_w"] = spread(np.tile(a["L1_attn_o_norm_w"], 8))
    w["a_log"] = spread(a["L1_attn_A_log"])
    w["dt_bias"] = spread(a["L1_attn_dt_bias"])
    w["wo1"] = rows(a["L1_attn_Wo"])
    w["eye"] = np.repeat(np.eye(P, dtype=np.float32)[:, None], 8, 1)
    i = np.arange(P)
    low = np.stack([(i[:, None] >> l == (i[None] >> l) + 1) & (i[None] >> (l + 1) == i[:, None] >> (l + 1)) for l in range(7)])
    w["joins"] = np.tile(np.stack([low, low.transpose(0, 2, 1)]), (1, 1, 1, 4)).astype(np.int32).transpose(2, 0, 1, 3)
    return {k: np.ascontiguousarray(v) for k, v in w.items()}


def kernel(**inputs):
    import concourse.bacc as bacc
    from concourse.bass_utils import run_bass_kernel_spmd

    nc = bacc.Bacc("TRN2", target_bir_lowering=False, num_devices=1)
    a = {name: np.asarray(value) for name, value in inputs.items()}
    arrays = {"x": np.ascontiguousarray(a["L0_attn_encodings"]), **layout(a)}
    aps = {name: nc.dram_tensor(name, m.shape, mybir.dt.from_np(m.dtype), kind="ExternalInput").ap() for name, m in arrays.items()}
    out = nc.dram_tensor("out", [8, 1024, 256], F32, kind="ExternalOutput").ap()
    two_layers(nc, aps["x"], aps, out)
    r = run_bass_kernel_spmd(nc, [arrays], core_ids=[0])
    return r.results[0]["out"]
```
